# Optimizing a Trainium2 kernel written in Bass

```python
import numpy as np
import jax
import jax.numpy as jnp

def _softmax(x, axis=-1):
    return jax.nn.softmax(x, axis=axis)

def _gelu(x):
    return jax.nn.gelu(x, approximate=True)

def _silu(x):
    return jax.nn.silu(x)

def _sigmoid(x):
    return jax.nn.sigmoid(x)

def _layernorm(x, axis=-1, eps=1e-05):
    m = jnp.mean(x, axis=axis, keepdims=True)
    v = jnp.var(x, axis=axis, keepdims=True)
    return (x - m) / jnp.sqrt(v + eps)

def _scatter_add(tgt, idx, src, axis=0):
    return tgt.at[idx].add(src)

def _segment_sum(src, seg, n):
    return jax.ops.segment_sum(src, seg, n)
kernel_name = 'mk_lm_tower_d1_tok_ids768_r4_7f8bb7'

def setup_inputs(seed: int=0):
    np.random.seed(seed)
    _w = jnp.asarray

    def _rec_inputs():
        import jax
        import jax.numpy as jnp
        _rk = jax.random.key(seed)
        x = jax.random.randint(jax.random.fold_in(_rk, 1), (4, 1024), 0, 31983, jnp.int32)
        return x
    x = _rec_inputs()

    def _L0_tok_setup():
        import jax, jax.numpy as jnp
        import numpy as np
        NUM_EMBEDDINGS = 8000
        EMBED_DIM = 192
        BATCH, POS = (2, 512)
        INIT_RANGE = 0.02
        key = jax.random.key(seed)
        kx, kw = jax.random.split(key)
        x = jax.random.randint(kx, (BATCH, POS), 0, NUM_EMBEDDINGS, dtype=jnp.int64 if jax.config.jax_enable_x64 else jnp.int32)
        W = jax.random.normal(kw, (NUM_EMBEDDINGS, EMBED_DIM), dtype=jnp.float32) * INIT_RANGE
        return {'x': x, 'W': W}
    _L0_tok_all = _L0_tok_setup()
    _L0_tok_in = {k: v for k, v in _L0_tok_all.items() if k in ('W',)}
    del _L0_tok_all

    def _L0_attn_setup():
        import jax, jax.numpy as jnp
        import numpy as np
        D_MODEL = 192
        EXPAND = 2
        D_INNER = EXPAND * D_MODEL
        N_STATE = 16
        D_CONV = 4
        DT_RANK = 48
        B, L = (2, 512)

        def _layernorm(x, w, b, eps=1e-05):
            mu = jnp.mean(x, axis=-1, keepdims=True)
            var = jnp.mean(jnp.square(x - mu), axis=-1, keepdims=True)
            return (x - mu) * jax.lax.rsqrt(var + eps) * w + b

        def _selective_scan(u, delta, A, Bm, Cm, Dv):
            deltaA = jnp.exp(delta[..., None] * A)
            deltaB_u = delta[..., None] * Bm[:, :, None, :] * u[..., None]

            def step(h, t):
                dA_t, dBu_t, C_t = t
                h = dA_t * h + dBu_t
                y = jnp.einsum('bdn,bn->bd', h, C_t)
                return (h, y)
            h0 = jnp.zeros(u.shape[:1] + A.shape, u.dtype)
            _, ys = jax.lax.scan(step, h0, (deltaA.transpose(1, 0, 2, 3), deltaB_u.transpose(1, 0, 2, 3), Cm.transpose(1, 0, 2)))
            y = ys.transpose(1, 0, 2)
            return y + u * Dv
        key = jax.random.key(seed)
        ks = jax.random.split(key, 10)
        g = lambda k, shape, s=0.02: jax.random.normal(k, shape, dtype=jnp.float32) * s
        A_log = jnp.log(jnp.tile(jnp.arange(1, N_STATE + 1, dtype=jnp.float32), (D_INNER, 1)))
        return {'x': jax.random.normal(ks[0], (B, L, D_MODEL), dtype=jnp.float32), 'ln_w': jnp.ones((D_MODEL,), jnp.float32), 'ln_b': jnp.zeros((D_MODEL,), jnp.float32), 'in_proj_w': g(ks[1], (2 * D_INNER, D_MODEL)), 'conv_w': g(ks[2], (D_INNER, 1, D_CONV), 0.2), 'conv_b': jnp.zeros((D_INNER,), jnp.float32), 'x_proj_w': g(ks[3], (DT_RANK + 2 * N_STATE, D_INNER)), 'dt_proj_w': g(ks[4], (D_INNER, DT_RANK), 0.1), 'dt_proj_b': g(ks[5], (D_INNER,), 0.5), 'A_log': A_log, 'D_param': jnp.ones((D_INNER,), jnp.float32), 'out_proj_w': g(ks[6], (D_MODEL, D_INNER))}
    _L0_attn_all = _L0_attn_setup()
    _L0_attn_in = {k: v for k, v in _L0_attn_all.items() if k in ('ln_w', 'ln_b', 'in_proj_w', 'conv_w', 'conv_b', 'x_proj_w', 'dt_proj_w', 'dt_proj_b', 'A_log', 'D_param', 'out_proj_w')}
    del _L0_attn_all

    def _L0_ffn_setup():
        import jax, jax.numpy as jnp
        import numpy as np
        D_MODEL, D_FF, N_EXPERTS, TOP_K = (192, 768, 8, 2)
        B, S = (2, 256)
        LN_EPS = 1e-05

        def _layernorm(x, gamma, beta):
            mu = jnp.mean(x, axis=-1, keepdims=True)
            var = jnp.mean(jnp.square(x - mu), axis=-1, keepdims=True)
            return (x - mu) * jax.lax.rsqrt(var + LN_EPS) * gamma + beta
        key = jax.random.key(seed)
        k1, k2, k3, k4 = jax.random.split(key, 4)
        return {'hidden_states': jax.random.normal(k1, (B, S, D_MODEL), dtype=jnp.float32), 'ln_gamma': jnp.ones((D_MODEL,), dtype=jnp.float32), 'ln_beta': jnp.zeros((D_MODEL,), dtype=jnp.float32), 'router_w': jax.random.normal(k2, (D_MODEL, N_EXPERTS), dtype=jnp.float32) * 0.02, 'w1': jax.random.normal(k3, (N_EXPERTS, D_MODEL, D_FF), dtype=jnp.float32) * 0.02, 'w2': jax.random.normal(k4, (N_EXPERTS, D_FF, D_MODEL), dtype=jnp.float32) * 0.02}
    _L0_ffn_all = _L0_ffn_setup()
    _L0_ffn_in = {k: v for k, v in _L0_ffn_all.items() if k in ('ln_gamma', 'ln_beta', 'router_w', 'w1', 'w2')}
    del _L0_ffn_all
    return {'x': x, 'L0_tok_W': _L0_tok_in['W'], 'L0_attn_ln_w': _L0_attn_in['ln_w'], 'L0_attn_ln_b': _L0_attn_in['ln_b'], 'L0_attn_in_proj_w': _L0_attn_in['in_proj_w'], 'L0_attn_conv_w': _L0_attn_in['conv_w'], 'L0_attn_conv_b': _L0_attn_in['conv_b'], 'L0_attn_x_proj_w': _L0_attn_in['x_proj_w'], 'L0_attn_dt_proj_w': _L0_attn_in['dt_proj_w'], 'L0_attn_dt_proj_b': _L0_attn_in['dt_proj_b'], 'L0_attn_A_log': _L0_attn_in['A_log'], 'L0_attn_D_param': _L0_attn_in['D_param'], 'L0_attn_out_proj_w': _L0_attn_in['out_proj_w'], 'L0_ffn_ln_gamma': _L0_ffn_in['ln_gamma'], 'L0_ffn_ln_beta': _L0_ffn_in['ln_beta'], 'L0_ffn_router_w': _L0_ffn_in['router_w'], 'L0_ffn_w1': _L0_ffn_in['w1'], 'L0_ffn_w2': _L0_ffn_in['w2']}

def reference(x, L0_tok_W, L0_attn_ln_w, L0_attn_ln_b, L0_attn_in_proj_w, L0_attn_conv_w, L0_attn_conv_b, L0_attn_x_proj_w, L0_attn_dt_proj_w, L0_attn_dt_proj_b, L0_attn_A_log, L0_attn_D_param, L0_attn_out_proj_w, L0_ffn_ln_gamma, L0_ffn_ln_beta, L0_ffn_router_w, L0_ffn_w1, L0_ffn_w2):
    import jax
    import jax.numpy as jnp

    def _L0_tok_ref(x, W):
        import jax, jax.numpy as jnp
        import numpy as np
        NUM_EMBEDDINGS = 8000
        EMBED_DIM = 192
        BATCH, POS = (2, 512)
        INIT_RANGE = 0.02
        onehot = jax.nn.one_hot(x, NUM_EMBEDDINGS, dtype=W.dtype)
        return jnp.einsum('bpn,nd->bpd', onehot, W)

    def _L0_attn_ref(x, ln_w, ln_b, in_proj_w, conv_w, conv_b, x_proj_w, dt_proj_w, dt_proj_b, A_log, D_param, out_proj_w):
        import jax, jax.numpy as jnp
        import numpy as np
        D_MODEL = 192
        EXPAND = 2
        D_INNER = EXPAND * D_MODEL
        N_STATE = 16
        D_CONV = 4
        DT_RANK = 48
        B, L = (2, 512)

        def _layernorm(x, w, b, eps=1e-05):
            mu = jnp.mean(x, axis=-1, keepdims=True)
            var = jnp.mean(jnp.square(x - mu), axis=-1, keepdims=True)
            return (x - mu) * jax.lax.rsqrt(var + eps) * w + b

        def _selective_scan(u, delta, A, Bm, Cm, Dv):
            deltaA = jnp.exp(delta[..., None] * A)
            deltaB_u = delta[..., None] * Bm[:, :, None, :] * u[..., None]

            def step(h, t):
                dA_t, dBu_t, C_t = t
                h = dA_t * h + dBu_t
                y = jnp.einsum('bdn,bn->bd', h, C_t)
                return (h, y)
            h0 = jnp.zeros(u.shape[:1] + A.shape, u.dtype)
            _, ys = jax.lax.scan(step, h0, (deltaA.transpose(1, 0, 2, 3), deltaB_u.transpose(1, 0, 2, 3), Cm.transpose(1, 0, 2)))
            y = ys.transpose(1, 0, 2)
            return y + u * Dv
        xn = _layernorm(x, ln_w, ln_b)
        xr = xn @ in_proj_w.T
        xin, res = jnp.split(xr, 2, axis=-1)
        xc = xin.transpose(0, 2, 1)
        xc = jax.lax.conv_general_dilated(xc, conv_w, window_strides=(1,), padding=[(D_CONV - 1, 0)], dimension_numbers=('NCH', 'OIH', 'NCH'), feature_group_count=D_INNER)
        xc = xc + conv_b[None, :, None]
        xin = jax.nn.silu(xc.transpose(0, 2, 1))
        A = -jnp.exp(A_log)
        dbc = xin @ x_proj_w.T
        dt, Bm, Cm = jnp.split(dbc, [DT_RANK, DT_RANK + N_STATE], axis=-1)
        delta = jax.nn.softplus(dt @ dt_proj_w.T + dt_proj_b)
        y = _selective_scan(xin, delta, A, Bm, Cm, D_param)
        y = y * jax.nn.silu(res)
        return y @ out_proj_w.T

    def _L0_ffn_ref(hidden_states, ln_gamma, ln_beta, router_w, w1, w2):
        import jax, jax.numpy as jnp
        import numpy as np
        D_MODEL, D_FF, N_EXPERTS, TOP_K = (192, 768, 8, 2)
        B, S = (2, 256)
        LN_EPS = 1e-05

        def _layernorm(x, gamma, beta):
            mu = jnp.mean(x, axis=-1, keepdims=True)
            var = jnp.mean(jnp.square(x - mu), axis=-1, keepdims=True)
            return (x - mu) * jax.lax.rsqrt(var + LN_EPS) * gamma + beta
        Bz, Sz, D = hidden_states.shape
        residual = hidden_states
        x = _layernorm(hidden_states, ln_gamma, ln_beta)
        tokens = x.reshape(-1, D)
        T = tokens.shape[0]
        logits = tokens @ router_w
        probs = jax.nn.softmax(logits, axis=-1)
        topw, topi = jax.lax.top_k(probs, TOP_K)
        topw = topw / jnp.sum(topw, axis=-1, keepdims=True)
        gates = jnp.zeros((T, N_EXPERTS), dtype=tokens.dtype)
        gates = gates.at[jnp.arange(T)[:, None], topi].set(topw)
        h = jnp.einsum('td,edf->etf', tokens, w1)
        h = jax.nn.silu(h)
        y = jnp.einsum('etf,efd->etd', h, w2)
        out = jnp.einsum('te,etd->td', gates, y)
        return residual + out.reshape(Bz, Sz, D)
    h = _L0_tok_ref(x, L0_tok_W)
    h = h + _L0_attn_ref(_layernorm(h, axis=-1), L0_attn_ln_w, L0_attn_ln_b, L0_attn_in_proj_w, L0_attn_conv_w, L0_attn_conv_b, L0_attn_x_proj_w, L0_attn_dt_proj_w, L0_attn_dt_proj_b, L0_attn_A_log, L0_attn_D_param, L0_attn_out_proj_w)
    h = h + _L0_ffn_ref(_layernorm(h, axis=-1), L0_ffn_ln_gamma, L0_ffn_ln_beta, L0_ffn_router_w, L0_ffn_w1, L0_ffn_w2)
    return h

_drawn_inputs = setup_inputs


def setup_inputs(seed=0):
    import zlib

    import numpy as np

    out = dict(_drawn_inputs(seed))
    spreads = {'L0_attn_ln_w': (1.0, 0.2),
     'L0_attn_ln_b': (0.0, 0.1),
     'L0_attn_conv_b': (0.0, 0.1),
     'L0_attn_D_param': (1.0, 0.2),
     'L0_ffn_ln_gamma': (1.0, 0.2),
     'L0_ffn_ln_beta': (0.0, 0.312)}
    factors = {'L0_attn_x_proj_w': 8.0,
     'L0_attn_dt_proj_w': 8.0,
     'L0_attn_dt_proj_b': 8.0,
     'L0_attn_A_log': 8.0}
    for name, (base, spread) in spreads.items():
        noise = np.random.default_rng([zlib.crc32(name.encode()), seed]).standard_normal(out[name].shape)
        drawn = base * np.exp(spread * noise) if base else spread * noise
        out[name] = jnp.asarray(drawn.astype(out[name].dtype))
    for name, factor in factors.items():
        out[name] = (out[name] * factor).astype(out[name].dtype)
    return out
```

```python
from contextlib import ExitStack

import numpy as np

import concourse.bass as bass
from concourse import mybir

F32 = mybir.dt.float32
BF16 = mybir.dt.bfloat16
U32 = mybir.dt.uint32
I32 = mybir.dt.int32
ALU = mybir.AluOpType
ACT = mybir.ActivationFunctionType
AX_X = mybir.AxisListType.X

P = 128
VOCAB = 8000
D = 192
DH = D - P
DI = 384
MT = DI // P
N = 16
TAPS = 4
R = 48
BATCH, SEQ = 4, 1024
TOK = BATCH * SEQ
CH = 512
TPC = CH // P
HALVES = SEQ // CH
NCH = TOK // CH
GT = TOK // P
DFF, E = 768, 8
FT = DFF // P
EPS = 1e-5
DT0, B0, C0, XR = 0, 64, 96, 112
CG = 4

U_TA, U_TB, U_IN, U_CONV, U_XP, U_DT, U_OUT = 0, 1, 2, 8, 11, 12, 15
USES = 17


def work_use(b, s, u):
    local = s * USES + u
    return local % 2, b * USES + local // 2


def settle(eng, passed):
    eng.sem_inc(passed, 1)


def mamba_moe(nc, ids, emb, c128, ident_d, sel_d, w_in, w_x, w_dt, w_out, router_w, w1, w2,
              rows, out, c_scratch):
    with ExitStack() as ctx:
        def sb(name, shape, dt=F32, stack=ctx):
            return stack.enter_context(nc.sbuf_tensor(name, shape, dt))

        def ps(name, shape, stack=ctx):
            return stack.enter_context(nc.psum_tensor(name, shape, F32))

        def sem(name):
            return ctx.enter_context(nc.semaphore(name))

        ids_sb = sb("ids_sb", [P, GT], I32)
        h_all = sb("h_all", [P, GT, D])
        ident = sb("ident", [P, P])
        eps = sb("eps", [P, 1])
        stats = sb("stats", [P, TPC, 6])
        mv = sb("mv", [P, TPC, 2])
        std = sb("std", [P, TPC])
        rstd = sb("rstd", [P, TPC])
        x1 = sb("x1", [P, TPC, D])
        x2 = sb("x2", [P, TPC, D])
        vec = sb("vec", [P, 11 + MT * (TAPS + 3 + N)])

        ids_in = sem("ids_in")
        passed = sem("passed")
        weights_in = sem("weights_in")
        h_zero = sem("h_zero")
        const_ready = sem("const_ready")
        gathered = sem("gathered")
        stats_done = sem("stats_done")
        aggr_done = sem("aggr_done")
        std_done = sem("std_done")
        rstd_done = sem("rstd_done")
        norm_done = sem("norm_done")

        ln_w, ln_b = (vec[:, 0:1], vec[0:DH, 1:2]), (vec[:, 2:3], vec[0:DH, 3:4])
        gamma, beta = (vec[:, 4:5], vec[0:DH, 5:6]), (vec[:, 6:7], vec[0:DH, 7:8])
        at = 11

        def cols(width):
            nonlocal at
            v = vec[:, at:at + MT * width].rearrange("p (m k) -> p m k", m=MT)
            at += MT * width
            return v

        conv_w, conv_b, dt_b, d_par, a_log = cols(TAPS), cols(1), cols(1), cols(1), cols(N)

        def layer_norm(dve, src, dst, k):
            for i in range(TPC):
                last = nc.vector.bn_stats(stats[:, i, :], src[i])
            last.then_inc(stats_done, 1)
            dve.wait_ge(stats_done, k + 1)
            settle(dve, passed)
            for i in range(TPC):
                last = nc.vector.bn_aggr(mv[:, i, :], stats[:, i, :])
            last.then_inc(aggr_done, 1)
            dve.wait_ge(std_done, k + 1)
            nc.vector.reciprocal(rstd[:, :], std[:, :]).then_inc(rstd_done, 1)
            dve.wait_ge(rstd_done, k + 1)
            for i in range(TPC):
                last = nc.vector.tensor_scalar(dst[i], src[i], mv[:, i, 0:1], rstd[:, i:i + 1],
                                               ALU.subtract, ALU.mult)
            last.then_inc(norm_done, 1)
            dve.wait_ge(norm_done, k + 1)

        def layer_norm_std(act, k):
            act.wait_ge(aggr_done, k + 1)
            nc.scalar.activation(std[:, :], mv[:, :, 1], ACT.Sqrt, bias=eps[:, 0:1]).then_inc(std_done, 1)

        with ExitStack() as mctx:
            w_in_a = sb("w_in_a", [P, 2 * DI], F32, mctx)
            w_in_b = sb("w_in_b", [DH, 2 * DI], F32, mctx)
            w_x_sb = sb("w_x_sb", [P, MT, XR], F32, mctx)
            w_dt_sb = sb("w_dt_sb", [R, DI], F32, mctx)
            w_out_sb = sb("w_out_sb", [P, MT, D], F32, mctx)
            sel = sb("sel", [96, N, P], BF16, mctx)
            a_neg = sb("a_neg", [P, MT, N], F32, mctx)
            a_exp = sb("a_exp", [P, MT, N], F32, mctx)
            conv_diag = sb("conv_diag", [P, MT, TAPS, P], F32, mctx)
            d_diag = sb("d_diag", [P, MT, P], F32, mctx)
            xn_a = sb("xn_a", [P, CH], F32, mctx)
            xn_b = sb("xn_b", [DH, CH], F32, mctx)
            xin = sb("xin", [P, MT, TAPS - 1 + SEQ], F32, mctx)
            gres = sb("gres", [P, MT, CH], F32, mctx)
            u_sb = sb("u_sb", [P, MT, CH], F32, mctx)
            dt_sb = sb("dt_sb", [R, CH], F32, mctx)
            bc_rows = sb("bc_rows", [N, CH], F32, mctx)
            c_rows = sb("c_rows", [N, CH], F32, mctx)
            b_hi = sb("b_hi", [N, 2, CH], BF16, mctx)
            b_rest = sb("b_rest", [N, 2, CH], F32, mctx)
            b_parts = sb("b_parts", [96, CH], BF16, mctx)
            sp_x = sb("sp_x", [P, MT, CH], F32, mctx)
            sp_nabs = sb("sp_nabs", [P, MT, CH], F32, mctx)
            sp_exp = sb("sp_exp", [P, MT, CH], F32, mctx)
            sp_one = sb("sp_one", [P, MT, CH], F32, mctx)
            sp_ln = sb("sp_ln", [P, MT, CH], F32, mctx)
            delta = sb("delta", [P, MT, CH], F32, mctx)
            du = sb("du", [P, MT, CH], F32, mctx)
            c_bc = sb("c_bc", [P, N, CH], F32, mctx)
            dbu = sb("dbu", [P, 2, MT, CH], F32, mctx)
            hst = sb("hst", [P, 2, MT, CH], F32, mctx)
            hc = sb("hc", [P, 2, MT, CH], F32, mctx)
            h_last = sb("h_last", [P, MT, N], F32, mctx)
            yg = sp_nabs

            work = [ps(f"work{k}", [P, CH], mctx) for k in range(2)]
            b_bc = ps("b_bc", [P, CH], mctx)
            decay = ps("decay", [P, 2, CH], mctx)
            y_ps = ps("y_ps", [P, MT, CH], mctx)

            filled = [sem(f"work_filled{k}") for k in range(2)]
            freed = [sem(f"work_freed{k}") for k in range(2)]
            diag_ready = sem("diag_ready")
            a_exp_done = sem("a_exp_done")
            a_ready = sem("a_ready")
            rows_ready = sem("rows_ready")
            split_step = sem("split_step")
            parts_ready = sem("parts_ready")
            c_stored = sem("c_stored")
            c_loaded = [sem(f"c_loaded{g}") for g in range(N // CG)]
            nabs_done = sem("nabs_done")
            exp_done = sem("exp_done")
            one_done = sem("one_done")
            ln_done = sem("ln_done")
            sp_step = sem("sp_step")
            delta_ready = sem("delta_ready")
            du_ready = sem("du_ready")
            b_bc_ready = sem("b_bc_ready")
            dbu_ready = sem("dbu_ready")
            decay_ready = sem("decay_ready")
            scanned = sem("scanned")
            last_saved = sem("last_saved")
            hc_ready = sem("hc_ready")
            hc_added = sem("hc_added")
            y_skip = sem("y_skip")
            y_done = sem("y_done")
            gated = sem("gated")
            chunk_done = sem("chunk_done")

            block = mctx.enter_context(nc.Block())

            @block.sync
            def _(sp):
                sp.dma_start(ids_sb[:, :], ids).then_inc(ids_in, 16)
                for dst, src in ((vec[:, :], c128), (ident[:, :], ident_d), (sel[:, :, :], sel_d),
                                 (w_in_a[:, :], w_in[0:P, :]), (w_in_b[:, :], w_in[P:D, :]),
                                 (w_x_sb[:, :, :], w_x.rearrange("(m p) r -> p m r", p=P)),
                                 (w_dt_sb[:, :], w_dt),
                                 (w_out_sb[:, :, :], w_out.rearrange("(m p) r -> p m r", p=P))):
                    sp.dma_start(dst, src).then_inc(weights_in, 16)
                with sp.Fori(0, BATCH) as b:
                    for s in range(HALVES):
                        c = b * HALVES + s
                        sp.wait_ge(rows_ready, 2 * c + 2)
                        sp.dma_start(c_scratch[s], c_rows[:, :]).then_inc(c_stored, 16)
                        sp.wait_ge(c_stored, 16 * c + 16)
                        for g in range(N // CG):
                            src = c_scratch[s:s + 1, g * CG:(g + 1) * CG, :].broadcast_to([P, CG, CH])
                            sp.dma_start(c_bc[:, g * CG:(g + 1) * CG, :], src).then_inc(c_loaded[g], 16)
                        sp.wait_ge(chunk_done, c + 1)
                        settle(sp, passed)

            @block.gpsimd
            def _(pool):
                pool.wait_ge(ids_in, 16)
                pool.wait_ge(h_zero, 1)
                for g in range(GT):
                    nc.gpsimd.indirect_dma_start(
                        h_all[:, g, :], None, emb, bass.IndirectOffsetOnAxis(ids_sb[:, g:g + 1].bitcast(U32), 0),
                        bounds_check=VOCAB - 1, oob_is_err=False).then_inc(gathered, 16)
                with pool.Fori(0, BATCH) as b:
                    for s in range(HALVES):
                        c = b * HALVES + s
                        for g in range(N // CG):
                            pool.wait_ge(c_loaded[g], 16 * c + 16)
                        settle(pool, passed)
                        with pool.Fori(0, N // 2) as n2_half:
                            n2 = n2_half * 2
                            for j in range(2):
                                q = c * N + n2 + j
                                pool.wait_ge(scanned, MT * (q + 1) + 2)
                                if s == 0:
                                    nc.gpsimd.tensor_copy(h_last[:, :, bass.ds(n2 + j, 1)],
                                                          hst[:, j, :, CH - 1:CH]).then_inc(last_saved, 1)
                                pool.wait_ge(hc_added, q + 1)
                                nc.gpsimd.tensor_tensor(
                                    hc[:, j, :, :], hst[:, j, :, :],
                                    c_bc[:, bass.ds(n2 + j, 1), :].broadcast_to([P, MT, CH]),
                                    ALU.mult).then_inc(hc_ready, 1)

            @block.scalar
            def _(act):
                act.wait_ge(weights_in, 16 * 8)
                act.wait_ge(const_ready, 1)
                nc.scalar.activation(a_exp[:, :, :], a_log, ACT.Exp).then_inc(a_exp_done, 1)
                act.wait_ge(a_exp_done, 1)
                nc.scalar.mul(a_neg[:, :, :], a_exp[:, :, :], -1.0).then_inc(a_ready, 1)
                act.wait_ge(a_ready, 1)

                with act.Fori(0, BATCH) as b:
                    for s in range(HALVES):
                        c = b * HALVES + s
                        layer_norm_std(act, 2 * c)
                        layer_norm_std(act, 2 * c + 1)

                        def evacuate(u, dst, func, r0=0, r1=P, **kw):
                            k, uses = work_use(b, s, u)
                            act.wait_ge(filled[k], uses + 1)
                            nc.scalar.activation(dst, work[k][r0:r1, :], func, **kw).then_inc(freed[k], 1)

                        evacuate(U_TA, xn_a[:, :], ACT.Identity, scale=ln_w[0], bias=ln_b[0])
                        evacuate(U_TB, xn_b[:, :], ACT.Identity, 0, DH, scale=ln_w[1], bias=ln_b[1])
                        for m in range(MT):
                            t0 = TAPS - 1 + s * CH
                            evacuate(U_IN + m, xin[:, m, t0:t0 + CH], ACT.Copy)
                        for m in range(MT):
                            evacuate(U_IN + MT + m, gres[:, m, :], ACT.Silu)
                        for m in range(MT):
                            evacuate(U_CONV + m, u_sb[:, m, :], ACT.Silu, bias=conv_b[:, m, :])
                        k, uses = work_use(b, s, U_XP)
                        act.wait_ge(filled[k], uses + 1)
                        nc.scalar.activation(bc_rows[:, :], work[k][B0:B0 + N, :], ACT.Copy).then_inc(rows_ready, 1)
                        nc.scalar.activation(c_rows[:, :], work[k][C0:C0 + N, :], ACT.Copy).then_inc(rows_ready, 1)
                        evacuate(U_XP, dt_sb[:, :], ACT.Copy, DT0, DT0 + R)
                        for m in range(MT):
                            evacuate(U_DT + m, sp_x[:, m, :], ACT.Identity, bias=dt_b[:, m, :])
                        act.wait_ge(nabs_done, c + 1)
                        nc.scalar.activation(sp_exp[:, :, :], sp_nabs[:, :, :], ACT.Exp).then_inc(exp_done, 1)
                        act.wait_ge(one_done, c + 1)
                        nc.scalar.activation(sp_ln[:, :, :], sp_one[:, :, :], ACT.Ln).then_inc(ln_done, 1)
                        act.wait_ge(delta_ready, c + 1)
                        with act.Fori(0, N // 2) as n2_half:
                            n2 = n2_half * 2
                            for j in range(2):
                                q = c * N + n2 + j
                                for m in range(MT):
                                    slot = (j * MT + m) % 2
                                    act.wait_ge(scanned, q * MT + m + 1)
                                    nc.scalar.activation(decay[:, slot, :], delta[:, m, :], ACT.Exp,
                                                         scale=a_neg[:, m, bass.ds(n2 + j, 1)])\
                                        .then_inc(decay_ready, 1)
                        act.wait_ge(chunk_done, c + 1)

            @block.tensor
            def _(pe):
                pe.wait_ge(weights_in, 16 * 8)
                pe.wait_ge(diag_ready, 1)

                with pe.Fori(0, BATCH) as b:
                    for s in range(HALVES):
                        c = b * HALVES + s

                        def claim(u):
                            k, uses = work_use(b, s, u)
                            pe.wait_ge(freed[k], uses + 1)
                            return k

                        def moved(u):
                            k, uses = work_use(b, s, u)
                            pe.wait_ge(freed[k], uses + 2)

                        pe.wait_ge(norm_done, 2 * c + 2)
                        for u, c0, rows_ in ((U_TA, 0, P), (U_TB, P, DH)):
                            k = claim(u)
                            settle(pe, passed)
                            for i in range(TPC):
                                mm = nc.tensor.transpose(work[k][0:rows_, i * P:(i + 1) * P],
                                                         x2[:, i, c0:c0 + rows_], ident[:, :])
                            mm.then_inc(filled[k], 1)
                        moved(U_TA)
                        moved(U_TB)
                        for m in range(2 * MT):
                            k = claim(U_IN + m)
                            nc.tensor.matmul(work[k][:, :], w_in_a[:, m * P:(m + 1) * P], xn_a[:, :],
                                             start=True, stop=False)
                            nc.tensor.matmul(work[k][:, :], w_in_b[:, m * P:(m + 1) * P], xn_b[:, :],
                                             start=False, stop=True).then_inc(filled[k], 1)
                        for m in range(MT):
                            moved(U_IN + m)
                            k = claim(U_CONV + m)
                            for tap in range(TAPS):
                                mm = nc.tensor.matmul(work[k][:, :], conv_diag[:, m, tap, :],
                                                      xin[:, m, s * CH + tap:s * CH + tap + CH],
                                                      start=(tap == 0), stop=(tap == TAPS - 1))
                            mm.then_inc(filled[k], 1)
                        k = claim(U_XP)
                        for m in range(MT):
                            moved(U_CONV + m)
                            mm = nc.tensor.matmul(work[k][0:XR, :], w_x_sb[:, m, :], u_sb[:, m, :],
                                                  start=(m == 0), stop=(m == MT - 1))
                        mm.then_inc(filled[k], 1)
                        moved(U_XP)
                        for m in range(MT):
                            k = claim(U_DT + m)
                            nc.tensor.matmul(work[k][:, :], w_dt_sb[:, m * P:(m + 1) * P], dt_sb[:, :],
                                             start=True, stop=True).then_inc(filled[k], 1)
                        for m in range(MT):
                            mm = nc.tensor.matmul(y_ps[:, m, :], d_diag[:, m, :], u_sb[:, m, :],
                                                  start=True, stop=False)
                        mm.then_inc(y_skip, 1)
                        pe.wait_ge(parts_ready, c + 1)

                        def broadcast_b(q, n):
                            pe.wait_ge(dbu_ready, q + 1)
                            nc.tensor.matmul(b_bc[:, :], sel[:, n, :] if isinstance(n, int)
                                             else sel[:, bass.ds(n, 1), :],
                                             b_parts[:, :], start=True, stop=True).then_inc(b_bc_ready, 1)

                        def add_to_y(q, j, last):
                            pe.wait_ge(hc_ready, q + 3)
                            for m in range(MT):
                                mm = nc.tensor.matmul(y_ps[:, m, :], ident[:, :], hc[:, j, m, :],
                                                      start=False, stop=last)
                            mm.then_inc(hc_added, 1)

                        q0 = c * N
                        broadcast_b(q0, 0)
                        settle(pe, passed)
                        with pe.Fori(0, (N - 2) // 2) as n2_half:
                            n2 = n2_half * 2
                            broadcast_b(q0 + n2 + 1, n2 + 1)
                            add_to_y(q0 + n2, 0, False)
                            broadcast_b(q0 + n2 + 2, n2 + 2)
                            add_to_y(q0 + n2 + 1, 1, False)
                        broadcast_b(q0 + N - 1, N - 1)
                        add_to_y(q0 + N - 2, 0, False)
                        add_to_y(q0 + N - 1, 1, True)
                        pe.wait_ge(gated, c + 1)
                        for pair in range(TPC // 2):
                            k = claim(U_OUT + pair)
                            for i in range(2):
                                t = (2 * pair + i) * P
                                for m in range(MT):
                                    mm = nc.tensor.matmul(work[k][:, i * D:(i + 1) * D], yg[:, m, t:t + P],
                                                          w_out_sb[:, m, :], start=(m == 0), stop=(m == MT - 1))
                            mm.then_inc(filled[k], 1)

            @block.vector
            def _(dve):
                nc.vector.memset(h_all[:, :, :], 0.0).then_inc(h_zero, 1)
                nc.vector.memset(b_parts[:, :], 0.0)
                nc.vector.memset(xin[:, :, 0:TAPS - 1], 0.0)
                nc.vector.memset(eps[:, :], EPS).then_inc(const_ready, 1)
                dve.wait_ge(weights_in, 16 * 8)
                for m in range(MT):
                    for tap in range(TAPS):
                        nc.vector.tensor_scalar(conv_diag[:, m, tap, :], ident[:, :], conv_w[:, m, tap:tap + 1],
                                                None, ALU.mult)
                    last = nc.vector.tensor_scalar(d_diag[:, m, :], ident[:, :], d_par[:, m, :], None, ALU.mult)
                last.then_inc(diag_ready, 1)
                for reads in (scanned, last_saved, hc_ready, hc_added):
                    nc.vector.sem_inc(reads, 2)
                for reads in (*freed, dbu_ready):
                    nc.vector.sem_inc(reads, 1)
                dve.wait_ge(gathered, 16 * GT)

                with dve.Fori(0, BATCH) as b:
                    for s in range(HALVES):
                        c = b * HALVES + s
                        src = [h_all[:, bass.ds(c * TPC + i, 1), :].rearrange("p a d -> p (a d)") for i in range(TPC)]
                        layer_norm(dve, src, [x1[:, i, :] for i in range(TPC)], 2 * c)
                        layer_norm(dve, [x1[:, i, :] for i in range(TPC)], [x2[:, i, :] for i in range(TPC)], 2 * c + 1)
                        dve.wait_ge(rows_ready, 2 * c + 1)
                        nc.vector.tensor_copy(b_hi[:, 0, :], bc_rows[:, :])
                        nc.vector.tensor_copy(b_parts[0:N, :], bc_rows[:, :]).then_inc(split_step, 1)
                        dve.wait_ge(split_step, 4 * c + 1)
                        nc.vector.tensor_tensor(b_rest[:, 0, :], bc_rows[:, :], b_hi[:, 0, :], ALU.subtract)\
                            .then_inc(split_step, 1)
                        dve.wait_ge(split_step, 4 * c + 2)
                        nc.vector.tensor_copy(b_hi[:, 1, :], b_rest[:, 0, :])
                        nc.vector.tensor_copy(b_parts[32:32 + N, :], b_rest[:, 0, :]).then_inc(split_step, 1)
                        dve.wait_ge(split_step, 4 * c + 3)
                        nc.vector.tensor_tensor(b_rest[:, 1, :], b_rest[:, 0, :], b_hi[:, 1, :], ALU.subtract)\
                            .then_inc(split_step, 1)
                        dve.wait_ge(split_step, 4 * c + 4)
                        nc.vector.tensor_copy(b_parts[64:64 + N, :], b_rest[:, 1, :]).then_inc(parts_ready, 1)
                        for m in range(MT):
                            k, uses = work_use(b, s, U_DT + m)
                            dve.wait_ge(freed[k], uses + 2)
                        nc.vector.scalar_tensor_tensor(sp_nabs[:, :, :], sp_x[:, :, :], -1.0, sp_x[:, :, :],
                                                       ALU.mult, ALU.min).then_inc(nabs_done, 1)
                        dve.wait_ge(exp_done, c + 1)
                        nc.vector.tensor_scalar(sp_one[:, :, :], sp_exp[:, :, :], 1.0, None, ALU.add)\
                            .then_inc(one_done, 1)
                        dve.wait_ge(one_done, c + 1)
                        nc.vector.scalar_tensor_tensor(sp_exp[:, :, :], sp_one[:, :, :], 1.0, sp_exp[:, :, :],
                                                       ALU.subtract, ALU.subtract).then_inc(sp_step, 1)
                        dve.wait_ge(sp_step, 2 * c + 1)
                        nc.vector.scalar_tensor_tensor(delta[:, :, :], sp_x[:, :, :], 0.0, sp_exp[:, :, :],
                                                       ALU.max, ALU.subtract).then_inc(sp_step, 1)
                        dve.wait_ge(ln_done, c + 1)
                        dve.wait_ge(sp_step, 2 * c + 2)
                        nc.vector.tensor_tensor(delta[:, :, :], delta[:, :, :], sp_ln[:, :, :], ALU.add)\
                            .then_inc(delta_ready, 1)
                        dve.wait_ge(delta_ready, c + 1)
                        nc.vector.tensor_tensor(du[:, :, :], delta[:, :, :], u_sb[:, :, :], ALU.mult)\
                            .then_inc(du_ready, 1)
                        dve.wait_ge(du_ready, c + 1)
                        if s == 1:
                            dve.wait_ge(last_saved, (b + 1) * N + 2)
                        settle(dve, passed)
                        with dve.Fori(0, N // 2) as n2_half:
                            n2 = n2_half * 2
                            for j in range(2):
                                q = c * N + n2 + j
                                dve.wait_ge(b_bc_ready, q + 1)
                                dve.wait_ge(scanned, q * MT + 1)
                                nc.vector.tensor_tensor(
                                    dbu[:, j, :, :], du[:, :, :],
                                    b_bc[:, :].rearrange("p (a t) -> p a t", a=1).broadcast_to([P, MT, CH]),
                                    ALU.mult).then_inc(dbu_ready, 1)
                                dve.wait_ge(dbu_ready, q + 2)
                                dve.wait_ge(hc_ready, q + 1)
                                if s == 0:
                                    dve.wait_ge(last_saved, b * N + n2 + j + 1)
                                for m in range(MT):
                                    slot = (j * MT + m) % 2
                                    dve.wait_ge(decay_ready, q * MT + m + 1)
                                    init = 0.0 if s == 0 else h_last[:, m, bass.ds(n2 + j, 1)]
                                    nc.vector.tensor_tensor_scan(hst[:, j, m, :], decay[:, slot, :], dbu[:, j, m, :],
                                                                 init, ALU.mult, ALU.add).then_inc(scanned, 1)
                        dve.wait_ge(hc_added, (c + 1) * N + 2)
                        nc.vector.tensor_tensor(yg[:, :, :], y_ps[:, :, :], gres[:, :, :], ALU.mult)\
                            .then_inc(gated, 1)
                        for pair in range(TPC // 2):
                            k, uses = work_use(b, s, U_OUT + pair)
                            dve.wait_ge(filled[k], uses + 1)
                            h = h_all[:, bass.ds(c * TPC + 2 * pair, 2), :]
                            nc.vector.tensor_tensor(h, h, work[k][:, 0:2 * D].rearrange("p (a d) -> p a d", a=2),
                                                    ALU.add).then_inc(freed[k], 1)
                        dve.wait_ge(freed[(s * USES + U_OUT + 1) % 2], work_use(b, s, U_OUT + 1)[1] + 2)
                        nc.vector.sem_inc(chunk_done, 1)

        with ExitStack() as fctx:
            x_a = sb("x_a", [P, TOK], F32, fctx)
            x_b = sb("x_b", [DH, TOK], F32, fctx)
            xc_a = sb("xc_a", [P, CH], F32, fctx)
            xc_b = sb("xc_b", [DH, CH], F32, fctx)
            router_a = sb("router_a", [P, E], F32, fctx)
            router_b = sb("router_b", [DH, E], F32, fctx)
            gates = sb("gates", [P, GT * E], F32, fctx)
            expert_no = sb("expert_no", [P, E], F32, fctx)
            top = sb("top", [P, TPC, 8], F32, fctx)
            top_i = sb("top_i", [P, TPC, 8], U32, fctx)
            top_f = sb("top_f", [P, TPC, 2], F32, fctx)
            top_w = sb("top_w", [P, TPC, 2], F32, fctx)
            lmax = sb("lmax", [P, TPC], F32, fctx)
            psum_ = sb("psum_", [P, TPC], F32, fctx)
            prob = sb("prob", [P, 3, TPC, E], F32, fctx)
            pick = sb("pick", [P, 2, TPC, E], F32, fctx)
            w1_a = sb("w1_a", [P, 2, DFF], F32, fctx)
            w1_b = sb("w1_b", [DH, 2, DFF], F32, fctx)
            w2_sb = sb("w2_sb", [P, 2, FT, D], F32, fctx)
            hid = sb("hid", [P, 2, FT, CH], F32, fctx)

            tr = [ps(f"tr{k}", [P, CH], fctx) for k in range(2)]
            lg = ps("lg", [P, CH], fctx)
            hp = [ps(f"hp{k}", [P, CH], fctx) for k in range(2)]
            yp = [ps(f"yp{k}", [P, CH], fctx) for k in range(2)]

            router_in = sem("router_in")
            residual_added = sem("residual_added")
            turned = sem("turned")
            xc_ready = sem("xc_ready")
            logits_done = sem("logits_done")
            x_kept = sem("x_kept")
            soft_step = sem("soft_step")
            prob_exp = sem("prob_exp")
            gates_done = sem("gates_done")
            w_in_sem = [sem(f"expert_in{k}") for k in range(2)]
            expert_done = sem("expert_done")
            hid_filled = sem("hid_filled")
            hid_silu = sem("hid_silu")
            y_filled = sem("y_filled")
            y_added = sem("y_added")
            stored = sem("stored")

            block2 = fctx.enter_context(nc.Block())
            PAIRS = TPC // 2

            @block2.sync
            def _(sp):
                sp.dma_start(router_a[:, :], router_w[0:P, :]).then_inc(router_in, 16)
                sp.dma_start(router_b[:, :], router_w[P:D, :]).then_inc(router_in, 16)

                def load_expert(e, k):
                    e_ = bass.ds(e, 1)
                    sp.dma_start(w1_a[:, k:k + 1, :], w1[e_, 0:P, :].rearrange("e d f -> d e f"))\
                        .then_inc(w_in_sem[k], 16)
                    sp.dma_start(w1_b[:, k:k + 1, :], w1[e_, P:D, :].rearrange("e d f -> d e f"))\
                        .then_inc(w_in_sem[k], 16)
                    sp.dma_start(w2_sb[:, k, :, :], w2[e_, :, :].rearrange("e (f p) d -> p (e f) d", p=P))\
                        .then_inc(w_in_sem[k], 16)

                load_expert(0, 0)
                load_expert(1, 1)
                with sp.Fori(1, E // 2) as e2_half:
                    e2 = e2_half * 2
                    for k in range(2):
                        sp.wait_ge(expert_done, e2 + k - 1)
                        load_expert(e2 + k, k)
                sp.wait_ge(y_added, E * NCH * PAIRS + 2)
                sp.dma_start(out.rearrange("(g p) d -> p g d", p=P), h_all[:, :, :]).then_inc(stored, 16)
                sp.wait_ge(stored, 16)

            @block2.gpsimd
            def _(pool):
                nc.gpsimd.iota(expert_no[:, :], [[1, E]], base=0, channel_multiplier=0,
                               allow_small_or_imprecise_dtypes=True).then_inc(x_kept, 1)
                with pool.Fori(0, NCH) as c:
                    pool.wait_ge(xc_ready, 2 * c + 3)
                    nc.gpsimd.tensor_copy(x_a[:, bass.ds(c * CH, CH)], xc_a[:, :])
                    nc.gpsimd.tensor_copy(x_b[:, bass.ds(c * CH, CH)], xc_b[:, :]).then_inc(x_kept, 1)

            @block2.scalar
            def _(act):
                with act.Fori(0, NCH) as c:
                    layer_norm_std(act, 2 * NCH + 2 * c)
                    layer_norm_std(act, 2 * NCH + 2 * c + 1)
                    act.wait_ge(x_kept, c + 1)
                    act.wait_ge(logits_done, c + 1)
                    for part, xc in enumerate((xc_a, xc_b)):
                        act.wait_ge(turned, 2 * c + part + 1)
                        nc.scalar.activation(xc[:, :], tr[part][0:xc.shape[0], :], ACT.Identity,
                                             scale=gamma[part], bias=beta[part]).then_inc(xc_ready, 1)
                    act.wait_ge(soft_step, 5 * c + 6)
                    nc.scalar.activation(prob[:, 1, :, :], prob[:, 0, :, :], ACT.Exp).then_inc(prob_exp, 1)
                with act.Fori(0, E * NCH // 2) as unit2_half:
                    unit2 = unit2_half * 2
                    for j in range(2):
                        for f in range(FT):
                            g = (unit2 + j) * FT + f
                            act.wait_ge(hid_filled, g + 1)
                            if f == 0:
                                act.wait_ge(y_added, (unit2 + j) * PAIRS + 1)
                            nc.scalar.activation(hid[:, j, f, :], hp[f % 2][:, :], ACT.Silu).then_inc(hid_silu, 1)

            @block2.tensor
            def _(pe):
                pe.wait_ge(router_in, 32)
                with pe.Fori(0, NCH) as c:
                    pe.wait_ge(norm_done, 2 * NCH + 2 * c + 2)
                    pe.wait_ge(xc_ready, 2 * c + 1)
                    settle(pe, passed)
                    for part, (c0, rows_) in enumerate(((0, P), (P, DH))):
                        for i in range(TPC):
                            mm = nc.tensor.transpose(tr[part][0:rows_, i * P:(i + 1) * P],
                                                     x2[:, i, c0:c0 + rows_], ident[:, :])
                        mm.then_inc(turned, 1)
                    pe.wait_ge(xc_ready, 2 * c + 3)
                    pe.wait_ge(soft_step, 5 * c + 1)
                    for i in range(TPC):
                        for part, (xc, rt) in enumerate(((xc_a, router_a), (xc_b, router_b))):
                            mm = nc.tensor.matmul(lg[:, i * E:(i + 1) * E], xc[:, i * P:(i + 1) * P], rt[:, :],
                                                  start=(part == 0), stop=(part == 1))
                    mm.then_inc(logits_done, 1)
                pe.wait_ge(x_kept, NCH + 1)
                with pe.Fori(0, E // 2) as e2_half:
                    e2 = e2_half * 2
                    for k in range(2):
                        pe.wait_ge(w_in_sem[k], e2_half * 48 + 48)
                        settle(pe, passed)
                        with pe.Fori(0, NCH // 2) as c2_half:
                            c2 = c2_half * 2
                            for j in range(2):
                                unit = (e2 + k) * NCH + c2 + j
                                t = bass.ds((c2 + j) * CH, CH)
                                for f in range(FT):
                                    pe.wait_ge(hid_silu, unit * FT + f + 1)
                                    nc.tensor.matmul(hp[f % 2][:, :], w1_a[:, k, f * P:(f + 1) * P], x_a[:, t],
                                                     start=True, stop=False)
                                    nc.tensor.matmul(hp[f % 2][:, :], w1_b[:, k, f * P:(f + 1) * P], x_b[:, t],
                                                     start=False, stop=True).then_inc(hid_filled, 1)
                                pe.wait_ge(hid_silu, (unit + 1) * FT + 2)
                                for pair in range(PAIRS):
                                    pe.wait_ge(y_added, unit * PAIRS + pair + 1)
                                    for i in range(2):
                                        t0 = (2 * pair + i) * P
                                        for f in range(FT):
                                            mm = nc.tensor.matmul(yp[pair][:, i * D:(i + 1) * D],
                                                                  hid[:, j, f, t0:t0 + P], w2_sb[:, k, f, :],
                                                                  start=(f == 0), stop=(f == FT - 1))
                                    mm.then_inc(y_filled, 1)
                        pe.wait_ge(y_added, (e2 + k + 1) * NCH * PAIRS + 2)
                        nc.tensor.sem_inc(expert_done, 1)

            @block2.vector
            def _(dve):
                for reads in (hid_silu, y_added):
                    nc.vector.sem_inc(reads, 2)
                nc.vector.sem_inc(logits_done, 1)
                nc.vector.sem_inc(xc_ready, 1)
                nc.vector.sem_inc(soft_step, 5)
                with dve.Fori(0, NCH) as c:
                    src = [h_all[:, bass.ds(c * TPC + i, 1), :].rearrange("p a d -> p (a d)") for i in range(TPC)]
                    layer_norm(dve, src, [x1[:, i, :] for i in range(TPC)], 2 * NCH + 2 * c)
                    h = h_all[:, bass.ds(c * TPC, TPC), :]
                    nc.vector.tensor_tensor(h, h, x1[:, :, :], ALU.add).then_inc(residual_added, 1)
                    layer_norm(dve, [x1[:, i, :] for i in range(TPC)], [x2[:, i, :] for i in range(TPC)],
                               2 * NCH + 2 * c + 1)
                    dve.wait_ge(logits_done, c + 2)
                    logits = lg[:, 0:TPC * E].rearrange("p (i e) -> p i e", e=E)
                    nc.vector.tensor_reduce(lmax[:, :], logits, AX_X, ALU.max).then_inc(gates_done, 1)
                    steps = 13
                    dve.wait_ge(gates_done, steps * c + 1)
                    nc.vector.tensor_tensor(prob[:, 0, :, :], logits,
                                            lmax[:, :].unsqueeze(2).broadcast_to([P, TPC, E]),
                                            ALU.subtract).then_inc(soft_step, 1)
                    dve.wait_ge(prob_exp, c + 1)
                    nc.vector.tensor_reduce(psum_[:, :], prob[:, 1, :, :], AX_X, ALU.add).then_inc(soft_step, 1)
                    dve.wait_ge(soft_step, 5 * c + 7)
                    nc.vector.reciprocal(lmax[:, :], psum_[:, :]).then_inc(soft_step, 1)
                    dve.wait_ge(soft_step, 5 * c + 8)
                    nc.vector.tensor_tensor(prob[:, 2, :, :], prob[:, 1, :, :],
                                            lmax[:, :].unsqueeze(2).broadcast_to([P, TPC, E]),
                                            ALU.mult).then_inc(soft_step, 1)
                    dve.wait_ge(soft_step, 5 * c + 9)
                    settle(dve, passed)
                    for i in range(TPC):
                        last = nc.vector.max(top[:, i, :], prob[:, 2, i, :])
                    last.then_inc(soft_step, 1)
                    dve.wait_ge(soft_step, 5 * c + 10)
                    settle(dve, passed)
                    for i in range(TPC):
                        last = nc.vector.max_index(top_i[:, i, :], top[:, i, :], prob[:, 2, i, :])
                    last.then_inc(gates_done, 1)
                    nc.vector.tensor_tensor(psum_[:, :], top[:, :, 0], top[:, :, 1], ALU.add).then_inc(gates_done, 1)
                    dve.wait_ge(gates_done, steps * c + 3)
                    nc.vector.tensor_copy(top_f[:, :, :], top_i[:, :, 0:2]).then_inc(gates_done, 1)
                    nc.vector.reciprocal(lmax[:, :], psum_[:, :]).then_inc(gates_done, 1)
                    dve.wait_ge(gates_done, steps * c + 5)
                    nc.vector.tensor_tensor(top_w[:, :, :], top[:, :, 0:2],
                                            lmax[:, :].unsqueeze(2).broadcast_to([P, TPC, 2]),
                                            ALU.mult).then_inc(gates_done, 1)
                    dve.wait_ge(gates_done, steps * c + 6)
                    for i in range(TPC):
                        for r in range(2):
                            last = nc.vector.tensor_scalar(pick[:, r, i, :], expert_no[:, :], top_f[:, i, r:r + 1],
                                                           top_w[:, i, r:r + 1], ALU.is_equal, ALU.mult)
                    last.then_inc(gates_done, 6)
                    dve.wait_ge(gates_done, steps * c + 12)
                    nc.vector.tensor_tensor(gates[:, bass.ds(c * TPC * E, TPC * E)],
                                            pick[:, 0, :, :].rearrange("p i e -> p (i e)"),
                                            pick[:, 1, :, :].rearrange("p i e -> p (i e)"),
                                            ALU.add).then_inc(gates_done, 1)
                dve.wait_ge(gates_done, steps * NCH)
                with dve.Fori(0, E) as e:
                    with dve.Fori(0, NCH) as c:
                        for pair in range(PAIRS):
                            y = (e * NCH + c) * PAIRS + pair
                            dve.wait_ge(y_filled, y + 1)
                            dve.wait_ge(y_added, y + 1)
                            for i in range(2):
                                g = c * TPC + 2 * pair + i
                                h = h_all[:, bass.ds(g, 1), :].rearrange("p a d -> p (a d)")
                                last = nc.vector.scalar_tensor_tensor(
                                    h, yp[pair][:, i * D:(i + 1) * D], gates[:, bass.ds(g * E + e, 1)], h,
                                    ALU.mult, ALU.add)
                            last.then_inc(y_added, 1)


def kernel(**inputs):
    import ml_dtypes
    import concourse.bacc as bacc
    from concourse.bass_utils import run_bass_kernel_spmd

    a = {k: np.asarray(v) for k, v in inputs.items()}

    def tiles(x, fill=P):
        x = x.reshape(x.shape[0], -1)
        return x.reshape(-1, P, x.shape[1]).transpose(1, 0, 2).reshape(P, -1)

    def halves(x):
        v = np.zeros((P, 2), np.float32)
        v[:, 0] = x[:P]
        v[:DH, 1] = x[P:]
        return v

    c128 = np.concatenate(
        [halves(a["L0_attn_ln_w"]), halves(a["L0_attn_ln_b"]), halves(a["L0_ffn_ln_gamma"]),
         halves(a["L0_ffn_ln_beta"]), np.zeros((P, 3), np.float32), tiles(a["L0_attn_conv_w"][:, 0, :]),
         tiles(a["L0_attn_conv_b"]), tiles(a["L0_attn_dt_proj_b"]), tiles(a["L0_attn_D_param"]),
         tiles(a["L0_attn_A_log"])], axis=1)
    xp = a["L0_attn_x_proj_w"].T
    w_x = np.zeros((DI, XR), np.float32)
    w_x[:, DT0:DT0 + R] = xp[:, 0:R]
    w_x[:, B0:B0 + N] = xp[:, R:R + N]
    w_x[:, C0:C0 + N] = xp[:, R + N:R + 2 * N]
    sel = np.zeros((96, N, P), ml_dtypes.bfloat16)
    for part in range(3):
        for n in range(N):
            sel[32 * part + n, n, :] = 1
    arrays = {
        "ids": a["x"].reshape(GT, P).T,
        "emb": a["L0_tok_W"],
        "c128": c128,
        "ident_d": np.eye(P, dtype=np.float32),
        "sel_d": sel,
        "w_in": a["L0_attn_in_proj_w"].T,
        "w_x": w_x,
        "w_dt": a["L0_attn_dt_proj_w"].T,
        "w_out": a["L0_attn_out_proj_w"].T,
        "router_w": a["L0_ffn_router_w"],
        "w1": a["L0_ffn_w1"],
        "w2": a["L0_ffn_w2"],
    }
    nc = bacc.Bacc("TRN2", target_bir_lowering=False, num_devices=1)
    fed, args = {}, []
    for name, x in arrays.items():
        fed[name] = np.ascontiguousarray(x)
        args.append(nc.dram_tensor(name, x.shape, mybir.dt.from_np(x.dtype), kind="ExternalInput").ap())
    out = nc.dram_tensor("out", (TOK, D), F32, kind="ExternalOutput").ap()
    c_scratch = nc.dram_tensor("c_scratch", (HALVES, N, CH), F32, kind="Internal").ap()
    mamba_moe(nc, *args, None, out, c_scratch)
    r = run_bass_kernel_spmd(nc, [fed], core_ids=[0])
    return r.results[0]["out"].reshape(BATCH, SEQ, D)
```

```python
from contextlib import ExitStack

import numpy as np

import concourse.bass as bass
from concourse import mybir

F32 = mybir.dt.float32
BF16 = mybir.dt.bfloat16
U32 = mybir.dt.uint32
I32 = mybir.dt.int32
ALU = mybir.AluOpType
ACT = mybir.ActivationFunctionType
AX_X = mybir.AxisListType.X

P = 128
VOCAB = 8000
D = 192
DH = D - P
DI = 384
MT = DI // P
N = 16
TAPS = 4
R = 48
BATCH, SEQ = 4, 1024
TOK = BATCH * SEQ
CH = 512
TPC = CH // P
HALVES = SEQ // CH
NCH = TOK // CH
GT = TOK // P
DFF, E = 768, 8
FT = DFF // P
EPS = 1e-5
DT0, B0, C0, XR = 0, 64, 96, 112
CG = 2

ROW_ID, ROW_W, ROW_E, ROW = D, D + 1, D + 3, D + 5
TS = 256
TT = TS // P
LIST = TOK + TS
PAD_ROW = E * LIST
NT = 40
assert (2 * TOK + E * (TS - 1)) // TS < NT and NT % 4 == 0
HALO = TAPS - 1
HS = 4
AHEAD = 3
PAST = 0x7FFFFFFF
EXP_LN = "natural_log_exp_and_others"

ORDER = ["pre TA", "pre TB", "post OUT0", "pre IN0", "post OUT1", "pre IN1", "pre IN2", "pre CONV0",
         "post TA", "post TB", "pre CONV1", "pre CONV2", "post LOGITS", "pre RES0", "pre XP", "pre RES1",
         "pre RES2", "pre DT0", "pre DT1", "pre DT2", "post RANKS"]
USES = len(ORDER)
PRE = [x[4:] for x in ORDER if x.startswith("pre ")]
POST = [x[5:] for x in ORDER if x.startswith("post ")]


def bank_of(b, i):
    return i % 2, b * USES + i // 2


def pre_use(b, r, what):
    if isinstance(b, int) and 2 * b + r < 2:
        return bank_of(0, (2 * b + r) * len(PRE) + PRE.index(what))
    return bank_of(b, 2 * len(PRE) + (r - 2) * USES + ORDER.index("pre " + what))


def post_use(b, r, what):
    if isinstance(b, int) and 2 * b + r >= NCH - 2:
        return bank_of(0, 2 * len(PRE) + (NCH - 2) * USES + (2 * b + r - NCH + 2) * len(POST) + POST.index(what))
    return bank_of(b, 2 * len(PRE) + r * USES + ORDER.index("post " + what))


def settle(eng, passed):
    eng.sem_inc(passed, 1)


def mamba_moe(nc, ids, emb, c128, ident_d, sel_d, before_d, w_in, w_x, w_dt, w_out, router_w, w1, w2,
              out, c_scratch, lists):
    with ExitStack() as ctx:
        def sb(name, shape, dt=F32, stack=ctx):
            return stack.enter_context(nc.sbuf_tensor(name, shape, dt))

        def ps(name, shape, stack=ctx):
            return stack.enter_context(nc.psum_tensor(name, shape, F32))

        def sem(name):
            return ctx.enter_context(nc.semaphore(name))

        ids_sb = sb("ids_sb", [P, GT], I32)
        h_all = sb("h_all", [P, GT + TPC, D])
        ident = sb("ident", [P, P])
        minus_half = sb("minus_half", [P, TPC])

        class Norm:

            def __init__(self, name):
                self.stats = sb(f"{name}_stats", [P, TPC, 6])
                self.mv = sb(f"{name}_mv", [P, TPC, 2])
                self.var_eps = sb(f"{name}_var_eps", [P, TPC])
                self.rstd = sb(f"{name}_rstd", [P, TPC])
                self.stats_done = sem(f"{name}_stats_done")
                self.aggr_done = sem(f"{name}_aggr_done")
                self.var_ready = sem(f"{name}_var_ready")
                self.rstd_done = sem(f"{name}_rstd_done")
                self.norm_done = sem(f"{name}_norm_done")

        pre_norm, post_norm = Norm("pre"), Norm("post")
        x1 = sb("x1", [P, TPC, D])
        vec = sb("vec", [P, 11 + MT * (TAPS + 3 + N)])

        te_f = sb("te_f", [P, NT])
        te_i = sb("te_i", [P, NT], I32)
        row_i = sb("row_i", [P, NT], I32)
        count_i = sb("count_i", [P, E], I32)
        pad = sb("pad", [P, TT, ROW])

        ids_in = sem("ids_in")
        pad_ready = sem("pad_ready")
        scattered = [sem(f"scattered{k}") for k in range(2)]
        table_ready = sem("table_ready")
        padded = sem("padded")
        passed = sem("passed")
        weights_in = sem("weights_in")
        h_zero = sem("h_zero")
        half_ready = sem("half_ready")
        pad_zero = sem("pad_zero")
        gathered = [sem(f"gathered{k}") for k in range(3)]

        ln_w, ln_b = (vec[:, 0:1], vec[0:DH, 1:2]), (vec[:, 2:3], vec[0:DH, 3:4])
        gamma, beta = (vec[:, 4:5], vec[0:DH, 5:6]), (vec[:, 6:7], vec[0:DH, 7:8])
        at = 11

        def cols(width):
            nonlocal at
            v = vec[:, at:at + MT * width].rearrange("p (m k) -> p m k", m=MT)
            at += MT * width
            return v

        conv_w, conv_b, dt_b, d_par, a_log = cols(TAPS), cols(1), cols(1), cols(1), cols(N)

        def layer_norm_stats(dve, w, src, k):
            for i in range(TPC):
                last = nc.vector.bn_stats(w.stats[:, i, :], src[i])
            last.then_inc(w.stats_done, 1)
            dve.wait_ge(w.stats_done, k + 1)
            settle(dve, passed)
            for i in range(TPC):
                last = nc.vector.bn_aggr(w.mv[:, i, :], w.stats[:, i, :])
            last.then_inc(w.aggr_done, 1)
            dve.wait_ge(w.aggr_done, k + 1)
            nc.vector.tensor_scalar(w.var_eps[:, :], w.mv[:, :, 1], EPS, None, ALU.add).then_inc(w.var_ready, 1)

        def layer_norm_power(pool, w, k):
            pool.wait_ge(w.var_ready, k + 1)
            nc.gpsimd.tensor_tensor(w.rstd[:, :], w.var_eps[:, :], minus_half[:, :], ALU.pow)\
                .then_inc(w.rstd_done, 1)

        def layer_norm_apply(dve, w, src, dst, k):
            dve.wait_ge(w.rstd_done, k + 1)
            for i in range(TPC):
                last = nc.vector.tensor_scalar(dst[i], src[i], w.mv[:, i, 0:1], w.rstd[:, i:i + 1],
                                               ALU.subtract, ALU.mult)
            last.then_inc(w.norm_done, 1)
            dve.wait_ge(w.norm_done, k + 1)

        with ExitStack() as mctx:
            w_in_a = sb("w_in_a", [P, 2 * DI], F32, mctx)
            w_in_b = sb("w_in_b", [DH, 2 * DI], F32, mctx)
            w_x_sb = sb("w_x_sb", [P, MT, XR], F32, mctx)
            w_dt_sb = sb("w_dt_sb", [R, DI], F32, mctx)
            w_out_sb = sb("w_out_sb", [P, MT, D], F32, mctx)
            sel = sb("sel", [96, N, P], BF16, mctx)
            a_neg = sb("a_neg", [P, MT, N], F32, mctx)
            a_exp = sb("a_exp", [P, MT, N], F32, mctx)
            conv_diag = sb("conv_diag", [P, MT, TAPS, P], F32, mctx)
            d_diag = sb("d_diag", [P, MT, P], F32, mctx)
            xn_a = sb("xn_a", [P, CH], F32, mctx)
            xn_b = sb("xn_b", [DH, CH], F32, mctx)
            xin = sb("xin", [P, MT, HALO + CH], F32, mctx)
            gres = sb("gres", [P, 2, MT, CH], F32, mctx)
            u_sb = sb("u_sb", [P, 2, MT, CH], F32, mctx)
            dt_sb = sb("dt_sb", [R, CH], F32, mctx)
            b_rows = sb("b_rows", [N, CH], F32, mctx)
            c_rows = sb("c_rows", [N, CH], F32, mctx)
            b_part = sb("b_part", [N, 2, CH], BF16, mctx)
            b_parts = sb("b_parts", [96, 2, CH], BF16, mctx)
            sp_one = sb("sp_one", [P, MT, CH], F32, mctx)
            delta = sb("delta", [P, 2, MT, CH], F32, mctx)
            du = sb("du", [P, 2, MT, CH], F32, mctx)
            c_bc = sb("c_bc", [P, 2, CG, CH], F32, mctx)
            dbu = sb("dbu", [P, 2, MT, CH], F32, mctx)
            hst = sb("hst", [P, 2, MT, CH], F32, mctx)
            hc = sb("hc", [P, HS, MT, CH], F32, mctx)
            h_last = sb("h_last", [P, MT, N], F32, mctx)
            yg = sp_one

            before = sb("before", [P, P], F32, mctx)
            ones = sb("ones", [P, P], F32, mctx)
            router_a = sb("router_a", [P, E], F32, mctx)
            router_b = sb("router_b", [DH, E], F32, mctx)
            expert_no = sb("expert_no", [P, E], F32, mctx)
            list_start = sb("list_start", [P, E], F32, mctx)
            token_no = sb("token_no", [P, GT], I32, mctx)
            x3 = sb("x3", [P, TPC, D], F32, mctx)
            row = sb("row", [P, 2, TPC, ROW], F32, mctx)
            xm_a = sb("xm_a", [P, CH], F32, mctx)
            xm_b = sb("xm_b", [DH, CH], F32, mctx)
            col = sb("col", [P, 4, TPC], F32, mctx)
            prob = sb("prob", [P, 3, TPC, E], F32, mctx)
            top = sb("top", [P, TPC, 8], F32, mctx)
            top_i = sb("top_i", [P, TPC, 8], U32, mctx)
            pick = sb("pick", [P, 3, TPC, E], F32, mctx)
            place = sb("place", [P, TPC, E], F32, mctx)
            placed = sb("placed", [P, 2, TPC, E], F32, mctx)
            slot_f = sb("slot_f", [P, 2, TPC], F32, mctx)
            slot = sb("slot", [P, 2, 2, TPC], U32, mctx)
            tile_no = sb("tile_no", [P, NT], F32, mctx)
            count = sb("count", [P, E], F32, mctx)
            fills = sb("fills", [P, E, TOK // TS], F32, mctx)
            tiles_of = sb("tiles_of", [P, E], F32, mctx)
            tile_end = sb("tile_end", [P, E], F32, mctx)
            fit = sb("fit", [P, NT, E], F32, mctx)
            row_f = sb("row_f", [P, NT], F32, mctx)
            idle = sb("idle", [P, NT], F32, mctx)
            run = sb("run", [P, GT + 1, E], F32, mctx)

            work = [ps(f"work{k}", [P, CH], mctx) for k in range(2)]
            b_bc = ps("b_bc", [P, CH], mctx)
            decay = ps("decay", [P, 2, CH], mctx)
            y_ps = ps("y_ps", [P, MT, CH], mctx)

            filled = [sem(f"work_filled{k}") for k in range(2)]
            freed = [sem(f"work_freed{k}") for k in range(2)]
            diag_ready = sem("diag_ready")
            a_exp_done = sem("a_exp_done")
            a_ready = sem("a_ready")
            halo_ready = sem("halo_ready")
            silu_done = sem("silu_done")
            rows_ready = sem("rows_ready")
            split_step = sem("split_step")
            parts_ready = sem("parts_ready")
            c_stored = sem("c_stored")
            c_loaded = [sem(f"c_loaded{k}") for k in range(2)]
            nabs_done = sem("nabs_done")
            exp_done = sem("exp_done")
            one_done = sem("one_done")
            ln_done = sem("ln_done")
            sp_step = sem("sp_step")
            delta_ready = sem("delta_ready")
            du_ready = sem("du_ready")
            b_bc_ready = sem("b_bc_ready")
            dbu_ready = sem("dbu_ready")
            decay_ready = sem("decay_ready")
            scanned = sem("scanned")
            last_saved = sem("last_saved")
            hc_ready = sem("hc_ready")
            hc_added = sem("hc_added")
            gated = sem("gated")
            iota_ready = sem("iota_ready")
            start_ready = sem("start_ready")
            residual_added = sem("residual_added")
            stored = sem("stored")
            soft_step = sem("soft_step")
            prob_exp = sem("prob_exp")
            top_step = sem("top_step")
            pick_step = sem("pick_step")
            picked = sem("picked")
            slot_step = sem("slot_step")
            rank_step = sem("rank_step")
            slots_ready = sem("slots_ready")
            table_step = sem("table_step")

            block = mctx.enter_context(nc.Block())

            def no(b, r):
                return b * 2 + r

            @block.sync
            def _(sp):
                sp.dma_start(ids_sb[:, :], ids).then_inc(ids_in, 16)
                for dst, src in ((vec[:, :], c128), (ident[:, :], ident_d), (sel[:, :, :], sel_d),
                                 (w_in_a[:, :], w_in[0:P, :]), (w_in_b[:, :], w_in[P:D, :]),
                                 (w_x_sb[:, :, :], w_x.rearrange("(m p) r -> p m r", p=P)),
                                 (w_dt_sb[:, :], w_dt), (before[:, :], before_d),
                                 (router_a[:, :], router_w[0:P, :]), (router_b[:, :], router_w[P:D, :]),
                                 (w_out_sb[:, :, :], w_out.rearrange("(m p) r -> p m r", p=P))):
                    sp.dma_start(dst, src).then_inc(weights_in, 16)

                def spread_c(b, r, first=False):
                    c, s = no(b, r), r % 2
                    sp.wait_ge(rows_ready, 2 * c + 2)
                    sp.dma_start(c_scratch[s], c_rows[:, :]).then_inc(c_stored, 16)
                    sp.wait_ge(c_stored, 16 * c + 16)
                    settle(sp, passed)
                    for g in range(N // CG):
                        if not (first and g < 2):
                            sp.wait_ge(hc_ready, c * N + (g - 1) * CG + 2)
                            settle(sp, passed)
                        src = c_scratch[s:s + 1, g * CG:(g + 1) * CG, :].broadcast_to([P, CG, CH])
                        sp.dma_start(c_bc[:, g % 2, :, :], src).then_inc(c_loaded[g % 2], 16)

                def store_residual(b, r):
                    c = no(b, r)
                    sp.wait_ge(residual_added, c + 1)
                    settle(sp, passed)
                    src = h_all[:, bass.ds(c * TPC, TPC), :]
                    sp.dma_start(out[bass.ds(c * CH, CH), :].rearrange("(g p) d -> p g d", p=P), src)\
                        .then_inc(stored, 16)

                spread_c(0, 0, first=True)
                with sp.Fori(0, BATCH - 1) as b:
                    spread_c(b, 1)
                    store_residual(b, 0)
                    spread_c(b, 2)
                    store_residual(b, 1)
                spread_c(BATCH - 1, 1)
                store_residual(BATCH - 1, 0)
                store_residual(BATCH - 1, 1)
                sp.wait_ge(stored, 16 * NCH)
                sp.wait_ge(pad_ready, 1)
                sp.dma_start(lists[PAD_ROW:PAD_ROW + TS, :].rearrange("(i p) d -> p i d", p=P), pad[:, :, :])\
                    .then_inc(padded, 16)
                sp.wait_ge(table_ready, 1)
                for e in range(E):
                    end = sp.value_load(count_i[0:1, e:e + 1], min_val=e * LIST, max_val=e * LIST + TOK)
                    sp.dma_start(lists[bass.ds(end, TS), :].rearrange("(i p) d -> p i d", p=P), pad[:, :, :])\
                        .then_inc(padded, 16)
                sp.wait_ge(padded, 16 * (E + 1))

            @block.gpsimd
            def _(pool):
                nc.gpsimd.memset(minus_half[:, :], -0.5).then_inc(half_ready, 1)
                nc.gpsimd.iota(expert_no[:, :], [[1, E]], base=0, channel_multiplier=0,
                               allow_small_or_imprecise_dtypes=True)
                nc.gpsimd.iota(list_start[:, :], [[LIST, E]], base=0, channel_multiplier=0,
                               allow_small_or_imprecise_dtypes=True)
                nc.gpsimd.iota(tile_no[:, :], [[TS, NT]], base=0, channel_multiplier=0,
                               allow_small_or_imprecise_dtypes=True)
                nc.gpsimd.iota(token_no[:, :], [[P, GT]], base=0, channel_multiplier=1).then_inc(iota_ready, 1)
                nc.gpsimd.memset(pad[:, :, :], 0.0).then_inc(pad_zero, 1)
                pool.wait_ge(pad_zero, 1)
                nc.gpsimd.iota(pad[:, :, ROW_ID:ROW_ID + 1].bitcast(I32), [[0, TT]], base=TOK, channel_multiplier=0)\
                    .then_inc(pad_ready, 1)
                pool.wait_ge(ids_in, 16)
                for g in range(GT):
                    if g in (0, TPC):
                        pool.wait_ge(h_zero, 1 if g == 0 else 2)
                    nc.gpsimd.indirect_dma_start(
                        h_all[:, g, :], None, emb, bass.IndirectOffsetOnAxis(ids_sb[:, g:g + 1].bitcast(U32), 0),
                        bounds_check=VOCAB - 1, oob_is_err=False).then_inc(gathered[min(g // TPC, 2)], 16)
                pool.wait_ge(half_ready, 1)
                for k in range(4):
                    layer_norm_power(pool, pre_norm, k)

                def scatter(b, r, k):
                    s, choice, i = r % 2, k // TPC, k % TPC
                    nc.gpsimd.indirect_dma_start(
                        lists, bass.IndirectOffsetOnAxis(slot[:, s, choice, i:i + 1], 0), row[:, s, i, :], None,
                        bounds_check=E * LIST - 1, oob_is_err=False).then_inc(scattered[s], 16)

                def scan_chunk(b, r, first=False, last=False):
                    c, s = no(b, r), r % 2
                    for n in range(N):
                        q = c * N + n
                        if n == 0 and not first:
                            pool.wait_ge(slots_ready, c)
                        if n % CG == 0:
                            g = n // CG
                            pool.wait_ge(c_loaded[g % 2], 16 * (N // CG // 2 * c + g // 2 + 1))
                            settle(pool, passed)
                        pool.wait_ge(scanned, MT * (q + 1) + 2)
                        if s == 0:
                            settle(pool, passed)
                            nc.gpsimd.tensor_copy(h_last[:, :, n:n + 1], hst[:, n % 2, :, CH - 1:CH])\
                                .then_inc(last_saved, 1)
                        pool.wait_ge(hc_added, q + 1)
                        nc.gpsimd.tensor_tensor(hc[:, n % HS, :, :], hst[:, n % 2, :, :],
                                                c_bc[:, (n // CG) % 2, n % CG:n % CG + 1, :].broadcast_to([P, MT, CH]),
                                                ALU.mult).then_inc(hc_ready, 1)
                        if not last and n in (5, 8):
                            layer_norm_power(pool, pre_norm, 2 * (c + 2) + (n == 8))
                        if not first and n in (3, 4):
                            layer_norm_power(pool, post_norm, 2 * (c - 1) + (n == 4))
                        if not first and 6 <= n < 14:
                            scatter(b, r - 2, n - 6)

                scan_chunk(0, 0, first=True)
                with pool.Fori(0, BATCH - 1) as b:
                    scan_chunk(b, 1)
                    scan_chunk(b, 2)
                scan_chunk(BATCH - 1, 1, last=True)
                pool.wait_ge(slots_ready, NCH)
                for k in range(2 * TPC):
                    scatter(BATCH - 1, 0, k)
                for step in range(2):
                    layer_norm_power(pool, post_norm, 2 * (NCH - 1) + step)
                pool.wait_ge(slots_ready, NCH + 1)
                for k in range(2 * TPC):
                    scatter(BATCH - 1, 1, k)
                pool.wait_ge(scattered[0], 16 * 2 * TPC * BATCH)
                pool.wait_ge(scattered[1], 16 * 2 * TPC * (BATCH + 1))

            @block.scalar
            def _(act):
                act.wait_ge(weights_in, 16 * 11)
                nc.scalar.preload_act_table_set(EXP_LN)
                nc.scalar.activation(a_exp[:, :, :], a_log, ACT.Exp).then_inc(a_exp_done, 1)
                act.wait_ge(a_exp_done, 1)
                nc.scalar.mul(a_neg[:, :, :], a_exp[:, :, :], -1.0).then_inc(a_ready, 1)
                act.wait_ge(a_ready, 1)

                def evacuate(b, r, u, dst, r0=0, r1=P, **kw):
                    k, uses = pre_use(b, r, u)
                    act.wait_ge(filled[k], uses + 1)
                    func = ACT.Identity if kw else ACT.Copy
                    nc.scalar.activation(dst, work[k][r0:r1, :], func, **kw).then_inc(freed[k], 1)

                def post_norm_out(b, r):
                    for what, dst, r1, part in (("TA", xm_a, P, 0), ("TB", xm_b, DH, 1)):
                        k, uses = post_use(b, r, what)
                        act.wait_ge(filled[k], uses + 1)
                        nc.scalar.activation(dst[:, :], work[k][0:r1, :], ACT.Identity,
                                             scale=gamma[part], bias=beta[part]).then_inc(freed[k], 1)

                def router_exp(b, r):
                    act.wait_ge(soft_step, 2 * no(b, r) + 2)
                    nc.scalar.activation(prob[:, 1, :, :], prob[:, 0, :, :], ACT.Exp).then_inc(prob_exp, 1)

                def norm_out(b, r):
                    evacuate(b, r, "TA", xn_a[:, :], scale=ln_w[0], bias=ln_b[0])
                    evacuate(b, r, "TB", xn_b[:, :], 0, DH, scale=ln_w[1], bias=ln_b[1])

                def xin_out(b, r, m):
                    if m == 0:
                        act.wait_ge(halo_ready, no(b, r) + 1)
                    evacuate(b, r, f"IN{m}", xin[:, m, HALO:HALO + CH])

                def gres_out(b, r, m):
                    evacuate(b, r, f"RES{m}", gres[:, r % 2, m, :])

                def conv_out(b, r, m):
                    evacuate(b, r, f"CONV{m}", u_sb[:, r % 2, m, :], bias=conv_b[:, m, :])

                def silus(b, r, gate_chunk):
                    k, uses = pre_use(b, r, "CONV2")
                    act.wait_ge(freed[k], uses + 2)
                    nc.scalar.activation(u_sb[:, r % 2, :, :], u_sb[:, r % 2, :, :], ACT.Silu).then_inc(silu_done, 1)
                    if gate_chunk:
                        nc.scalar.activation(gres[:, 1 - r % 2, :, :], gres[:, 1 - r % 2, :, :], ACT.Silu)\
                            .then_inc(silu_done, 1)
                    nc.scalar.preload_act_table_set(EXP_LN)

                def rows_out(b, r):
                    c = no(b, r)
                    k, uses = pre_use(b, r, "XP")
                    act.wait_ge(filled[k], uses + 1)
                    nc.scalar.activation(b_rows[:, :], work[k][B0:B0 + N, :], ACT.Copy).then_inc(rows_ready, 1)
                    if not (isinstance(c, int) and c == 0):
                        act.wait_ge(c_stored, 16 * c)
                    nc.scalar.activation(c_rows[:, :], work[k][C0:C0 + N, :], ACT.Copy).then_inc(rows_ready, 1)
                    evacuate(b, r, "XP", dt_sb[:, :], DT0, DT0 + R)

                def dt_out(b, r):
                    for m in range(MT):
                        evacuate(b, r, f"DT{m}", delta[:, r % 2, m, :], bias=dt_b[:, m, :])

                def softplus_exp(b, r):
                    act.wait_ge(nabs_done, no(b, r) + 1)
                    nc.scalar.activation(du[:, r % 2, :, :], du[:, r % 2, :, :], ACT.Exp).then_inc(exp_done, 1)

                def softplus_ln(b, r):
                    act.wait_ge(sp_step, 2 * no(b, r) + 1)
                    nc.scalar.activation(sp_one[:, :, :], sp_one[:, :, :], ACT.Ln).then_inc(ln_done, 1)

                def scan_chunk(b, r, first=False, last=False):
                    c, s = no(b, r), r % 2
                    act.wait_ge(delta_ready, c + 1)
                    for n in range(N):
                        for m in range(MT):
                            i = (c * N + n) * MT + m
                            act.wait_ge(scanned, i + 1)
                            nc.scalar.activation(decay[:, (n * MT + m) % 2, :], delta[:, s, m, :], ACT.Exp,
                                                 scale=a_neg[:, m, n:n + 1]).then_inc(decay_ready, 1)
                        if last and n == 3:
                            nc.scalar.activation(gres[:, s, :, :], gres[:, s, :, :], ACT.Silu).then_inc(silu_done, 1)
                            nc.scalar.preload_act_table_set(EXP_LN)
                        if not first and n == 8:
                            post_norm_out(b, r - 1)
                        if not first and n == 11:
                            router_exp(b, r - 1)
                        if last:
                            continue
                        if n == 3:
                            norm_out(b, r + 1)
                        if n in (4, 5, 6):
                            xin_out(b, r + 1, n - 4)
                        if n in (7, 8, 9):
                            conv_out(b, r + 1, n - 7)
                        if n == 9:
                            silus(b, r + 1, True)
                        if n == 10:
                            gres_out(b, r + 1, 0)
                        if n == 11:
                            rows_out(b, r + 1)
                            gres_out(b, r + 1, 1)
                        if n == 12:
                            gres_out(b, r + 1, 2)
                        if n == 13:
                            dt_out(b, r + 1)
                        if n == 14:
                            softplus_exp(b, r + 1)
                        if n == 15:
                            softplus_ln(b, r + 1)

                norm_out(0, 0)
                for m in range(MT):
                    xin_out(0, 0, m)
                for m in range(MT):
                    conv_out(0, 0, m)
                silus(0, 0, False)
                gres_out(0, 0, 0)
                rows_out(0, 0)
                gres_out(0, 0, 1)
                gres_out(0, 0, 2)
                dt_out(0, 0)
                softplus_exp(0, 0)
                softplus_ln(0, 0)
                scan_chunk(0, 0, first=True)
                with act.Fori(0, BATCH - 1) as b:
                    scan_chunk(b, 1)
                    scan_chunk(b, 2)
                scan_chunk(BATCH - 1, 1, last=True)
                post_norm_out(BATCH - 1, 1)
                router_exp(BATCH - 1, 1)

            @block.tensor
            def _(pe):
                pe.wait_ge(weights_in, 16 * 11)
                pe.wait_ge(diag_ready, 1)

                def claim(use):
                    k, uses = use
                    pe.wait_ge(freed[k], uses + 1)
                    return k

                def moved(b, r, u):
                    k, uses = pre_use(b, r, u)
                    pe.wait_ge(freed[k], uses + 2)

                def turn(b, r):
                    pe.wait_ge(pre_norm.norm_done, 2 * no(b, r) + 2)
                    for u, c0, rows in (("TA", 0, P), ("TB", P, DH)):
                        k = claim(pre_use(b, r, u))
                        settle(pe, passed)
                        for i in range(TPC):
                            mm = nc.tensor.transpose(work[k][0:rows, i * P:(i + 1) * P],
                                                     x1[:, i, c0:c0 + rows], ident[:, :])
                        mm.then_inc(filled[k], 1)

                def project_in(b, r, u, m):
                    if u == "IN0":
                        moved(b, r, "TA")
                        moved(b, r, "TB")
                    k = claim(pre_use(b, r, u))
                    nc.tensor.matmul(work[k][:, :], w_in_a[:, m * P:(m + 1) * P], xn_a[:, :], start=True, stop=False)
                    nc.tensor.matmul(work[k][:, :], w_in_b[:, m * P:(m + 1) * P], xn_b[:, :], start=False, stop=True)\
                        .then_inc(filled[k], 1)

                def convolve(b, r, m):
                    moved(b, r, f"IN{m}")
                    k = claim(pre_use(b, r, f"CONV{m}"))
                    for tap in range(TAPS):
                        mm = nc.tensor.matmul(work[k][:, :], conv_diag[:, m, tap, :], xin[:, m, tap:tap + CH],
                                              start=(tap == 0), stop=(tap == TAPS - 1))
                    mm.then_inc(filled[k], 1)

                def project_x(b, r):
                    c = no(b, r)
                    pe.wait_ge(silu_done, 2 * c + 1)
                    k = claim(pre_use(b, r, "XP"))
                    for m in range(MT):
                        mm = nc.tensor.matmul(work[k][0:XR, :], w_x_sb[:, m, :], u_sb[:, r % 2, m, :],
                                              start=(m == 0), stop=(m == MT - 1))
                    mm.then_inc(filled[k], 1)

                def project_dt(b, r):
                    moved(b, r, "XP")
                    for m in range(MT):
                        k = claim(pre_use(b, r, f"DT{m}"))
                        nc.tensor.matmul(work[k][:, :], w_dt_sb[:, m * P:(m + 1) * P], dt_sb[:, :],
                                         start=True, stop=True).then_inc(filled[k], 1)

                def post_turn(b, r):
                    pe.wait_ge(post_norm.norm_done, 2 * no(b, r) + 2)
                    for what, c0, rows in (("TA", 0, P), ("TB", P, DH)):
                        k = claim(post_use(b, r, what))
                        settle(pe, passed)
                        for i in range(TPC):
                            mm = nc.tensor.transpose(work[k][0:rows, i * P:(i + 1) * P],
                                                     row[:, r % 2, i, c0:c0 + rows], ident[:, :])
                        mm.then_inc(filled[k], 1)

                def route(b, r):
                    for what in ("TA", "TB"):
                        k, uses = post_use(b, r, what)
                        pe.wait_ge(freed[k], uses + 2)
                    k = claim(post_use(b, r, "LOGITS"))
                    for i in range(TPC):
                        for part, (xm, rt) in enumerate(((xm_a, router_a), (xm_b, router_b))):
                            mm = nc.tensor.matmul(work[k][:, i * E:(i + 1) * E], xm[:, i * P:(i + 1) * P], rt[:, :],
                                                  start=(part == 0), stop=(part == 1))
                    mm.then_inc(filled[k], 1)

                def rank(b, r):
                    pe.wait_ge(picked, no(b, r) + 1)
                    k = claim(post_use(b, r, "RANKS"))
                    both = pick[:, 2, :, :].rearrange("p i e -> p (i e)")
                    nc.tensor.matmul(work[k][:, 0:TPC * E], before[:, :], both, start=True, stop=True)
                    nc.tensor.matmul(work[k][:, TPC * E:2 * TPC * E], ones[:, :], both, start=True, stop=True)\
                        .then_inc(filled[k], 1)

                def project_out(b, r, pair):
                    pe.wait_ge(gated, no(b, r) + 1)
                    k = claim(post_use(b, r, f"OUT{pair}"))
                    for i in range(2):
                        t = (2 * pair + i) * P
                        for m in range(MT):
                            mm = nc.tensor.matmul(work[k][:, i * D:(i + 1) * D], yg[:, m, t:t + P],
                                                  w_out_sb[:, m, :], start=(m == 0), stop=(m == MT - 1))
                    mm.then_inc(filled[k], 1)

                def broadcast_b(b, r, n):
                    if n >= N:
                        r, n = r + 1, n - N
                    c = no(b, r)
                    if n == 0:
                        pe.wait_ge(parts_ready, c + 1)
                    pe.wait_ge(dbu_ready, c * N + n + 1)
                    nc.tensor.matmul(b_bc[:, :], sel[:, n, :], b_parts[:, r % 2, :], start=True, stop=True)\
                        .then_inc(b_bc_ready, 1)

                def skip(b, r):
                    c = no(b, r)
                    if not (isinstance(c, int) and c == 0):
                        pe.wait_ge(gated, c)
                    for m in range(MT):
                        nc.tensor.matmul(y_ps[:, m, :], d_diag[:, m, :], u_sb[:, r % 2, m, :], start=True, stop=False)

                def scan_chunk(b, r, first=False, last=False):
                    c = no(b, r)
                    if first:
                        for n in range(AHEAD):
                            broadcast_b(b, r, n)
                    for n in range(N):
                        if n == 0:
                            broadcast_b(b, r, AHEAD)
                            skip(b, r)
                        pe.wait_ge(hc_ready, c * N + n + 3)
                        for m in range(MT):
                            mm = nc.tensor.matmul(y_ps[:, m, :], ident[:, :], hc[:, n % HS, m, :],
                                                  start=False, stop=(n == N - 1))
                        mm.then_inc(hc_added, 1)
                        if n > 0 and not (last and n + AHEAD >= N):
                            broadcast_b(b, r, n + AHEAD)
                        if not last and n == 0:
                            turn(b, r + 1)
                        if not first and n in (1, 2):
                            project_out(b, r - 1, n - 1)
                        if not last and n in (1, 2, 3):
                            project_in(b, r + 1, f"IN{n - 1}", n - 1)
                        if not last and n == 4:
                            convolve(b, r + 1, 0)
                        if not first and n == 5:
                            post_turn(b, r - 1)
                        if not last and n in (5, 6):
                            convolve(b, r + 1, n - 4)
                        if not first and n == 7:
                            route(b, r - 1)
                        if not last and n == 7:
                            project_in(b, r + 1, "RES0", MT)
                        if not last and n == 8:
                            project_x(b, r + 1)
                            project_in(b, r + 1, "RES1", MT + 1)
                        if not last and n == 9:
                            project_in(b, r + 1, "RES2", MT + 2)
                        if not last and n == 10:
                            project_dt(b, r + 1)
                        if not first and n == 11:
                            rank(b, r - 1)

                turn(0, 0)
                for m in range(MT):
                    project_in(0, 0, f"IN{m}", m)
                for m in range(MT):
                    convolve(0, 0, m)
                project_in(0, 0, "RES0", MT)
                project_x(0, 0)
                project_in(0, 0, "RES1", MT + 1)
                project_in(0, 0, "RES2", MT + 2)
                project_dt(0, 0)
                scan_chunk(0, 0, first=True)
                with pe.Fori(0, BATCH - 1) as b:
                    scan_chunk(b, 1)
                    scan_chunk(b, 2)
                scan_chunk(BATCH - 1, 1, last=True)
                for pair in range(TPC // 2):
                    project_out(BATCH - 1, 1, pair)
                post_turn(BATCH - 1, 1)
                route(BATCH - 1, 1)
                rank(BATCH - 1, 1)

            @block.vector
            def _(dve):
                nc.vector.memset(h_all[:, 0:TPC, :], 0.0).then_inc(h_zero, 1)
                nc.vector.memset(h_all[:, TPC:, :], 0.0).then_inc(h_zero, 1)
                nc.vector.memset(ones[:, :], 1.0)
                nc.vector.memset(row[:, :, :, :], 0.0)
                nc.vector.memset(slot[:, :, :, :], PAST).then_inc(slots_ready, 1)
                dve.wait_ge(iota_ready, 1)
                nc.vector.tensor_copy(run[:, 0, :], list_start[:, :]).then_inc(start_ready, 1)
                dve.wait_ge(start_ready, 1)
                nc.vector.memset(b_parts[:, :, :], 0.0)
                nc.vector.memset(xin[:, :, 0:HALO], 0.0).then_inc(halo_ready, 1)
                for reads in (scanned, last_saved, hc_ready):
                    nc.vector.sem_inc(reads, 2)
                nc.vector.sem_inc(hc_added, HS)
                for reads in (*freed, dbu_ready):
                    nc.vector.sem_inc(reads, 1)
                dve.wait_ge(weights_in, 16 * 11)
                for m in range(MT):
                    for tap in range(TAPS):
                        nc.vector.tensor_scalar(conv_diag[:, m, tap, :], ident[:, :], conv_w[:, m, tap:tap + 1],
                                                None, ALU.mult)
                    last_diag = nc.vector.tensor_scalar(d_diag[:, m, :], ident[:, :], d_par[:, m, :], None, ALU.mult)
                last_diag.then_inc(diag_ready, 1)

                x1_tiles = [x1[:, i, :] for i in range(TPC)]

                def norm_source(b, r):
                    return [h_all[:, bass.ds((no(b, r)) * TPC + i, 1), :].rearrange("p a d -> p (a d)")
                            if not isinstance(b, int) else h_all[:, no(b, r) * TPC + i, :] for i in range(TPC)]

                def norm_stats(b, r, step):
                    layer_norm_stats(dve, pre_norm, norm_source(b, r) if step == 0 else x1_tiles, 2 * no(b, r) + step)

                def norm_apply(b, r, step):
                    if step == 0 and not (isinstance(b, int) and no(b, r) == 0):
                        pb, pr = (b, r - 1)
                        k, uses = pre_use(pb, pr, "TB")
                        dve.wait_ge(filled[k], uses + 1)
                    layer_norm_apply(dve, pre_norm, norm_source(b, r) if step == 0 else x1_tiles, x1_tiles,
                                     2 * no(b, r) + step)

                def next_halo(b, r):
                    k, uses = pre_use(b, r - 1, "CONV2")
                    dve.wait_ge(filled[k], uses + 1)
                    settle(dve, passed)
                    if r % 2:
                        nc.vector.tensor_copy(xin[:, :, 0:HALO], xin[:, :, CH:CH + HALO]).then_inc(halo_ready, 1)
                    else:
                        nc.vector.memset(xin[:, :, 0:HALO], 0.0).then_inc(halo_ready, 1)

                def split_b(b, r):
                    c, s = no(b, r), r % 2
                    dve.wait_ge(rows_ready, 2 * c + 1)
                    nc.vector.tensor_copy(b_part[:, 0, :], b_rows[:, :])
                    nc.vector.tensor_copy(b_parts[0:N, s, :], b_rows[:, :]).then_inc(split_step, 1)
                    dve.wait_ge(split_step, 4 * c + 1)
                    nc.vector.tensor_tensor(b_rows[:, :], b_rows[:, :], b_part[:, 0, :], ALU.subtract)\
                        .then_inc(split_step, 1)
                    dve.wait_ge(split_step, 4 * c + 2)
                    nc.vector.tensor_copy(b_part[:, 1, :], b_rows[:, :])
                    nc.vector.tensor_copy(b_parts[32:32 + N, s, :], b_rows[:, :]).then_inc(split_step, 1)
                    dve.wait_ge(split_step, 4 * c + 3)
                    nc.vector.tensor_tensor(b_rows[:, :], b_rows[:, :], b_part[:, 1, :], ALU.subtract)\
                        .then_inc(split_step, 1)
                    dve.wait_ge(split_step, 4 * c + 4)
                    nc.vector.tensor_copy(b_parts[64:64 + N, s, :], b_rows[:, :]).then_inc(parts_ready, 1)

                def softplus_abs(b, r):
                    c, s = no(b, r), r % 2
                    for m in range(MT):
                        k, uses = pre_use(b, r, f"DT{m}")
                        dve.wait_ge(freed[k], uses + 2)
                    nc.vector.scalar_tensor_tensor(du[:, s, :, :], delta[:, s, :, :], -1.0, delta[:, s, :, :],
                                                   ALU.mult, ALU.min).then_inc(nabs_done, 1)

                def softplus_mid(b, r):
                    c, s = no(b, r), r % 2
                    dve.wait_ge(exp_done, c + 1)
                    nc.vector.tensor_scalar(sp_one[:, :, :], du[:, s, :, :], 1.0, None, ALU.add).then_inc(one_done, 1)
                    dve.wait_ge(one_done, c + 1)
                    nc.vector.scalar_tensor_tensor(du[:, s, :, :], sp_one[:, :, :], 1.0, du[:, s, :, :],
                                                   ALU.subtract, ALU.subtract).then_inc(sp_step, 1)
                    dve.wait_ge(sp_step, 2 * c + 1)
                    nc.vector.scalar_tensor_tensor(delta[:, s, :, :], delta[:, s, :, :], 0.0, du[:, s, :, :],
                                                   ALU.max, ALU.subtract).then_inc(sp_step, 1)

                def softplus_end(b, r):
                    c, s = no(b, r), r % 2
                    dve.wait_ge(ln_done, c + 1)
                    dve.wait_ge(sp_step, 2 * c + 2)
                    nc.vector.tensor_tensor(delta[:, s, :, :], delta[:, s, :, :], sp_one[:, :, :], ALU.add)\
                        .then_inc(delta_ready, 1)
                    dve.wait_ge(delta_ready, c + 1)
                    dve.wait_ge(silu_done, 2 * c + 1)
                    nc.vector.tensor_tensor(du[:, s, :, :], delta[:, s, :, :], u_sb[:, s, :, :], ALU.mult)\
                        .then_inc(du_ready, 1)

                def post_norm_source(b, r):
                    if isinstance(b, int):
                        return [h_all[:, no(b, r) * TPC + i, :] for i in range(TPC)]
                    return [h_all[:, bass.ds(no(b, r) * TPC + i, 1), :].rearrange("p a d -> p (a d)")
                            for i in range(TPC)]

                def post_norm_first(b, r):
                    for pair in range(TPC // 2):
                        k, uses = post_use(b, r, f"OUT{pair}")
                        dve.wait_ge(freed[k], uses + 2)
                    settle(dve, passed)
                    layer_norm_stats(dve, post_norm, post_norm_source(b, r), 2 * no(b, r))

                def post_norm_mid(b, r):
                    c = no(b, r)
                    x3_tiles = [x3[:, i, :] for i in range(TPC)]
                    layer_norm_apply(dve, post_norm, post_norm_source(b, r), x3_tiles, 2 * c)
                    h = h_all[:, bass.ds(c * TPC, TPC), :]
                    nc.vector.tensor_tensor(h, h, x3[:, :, :], ALU.add).then_inc(residual_added, 1)
                    layer_norm_stats(dve, post_norm, x3_tiles, 2 * c + 1)

                def post_norm_last(b, r):
                    c, s = no(b, r), r % 2
                    if not (isinstance(c, int) and c == 0):
                        dve.wait_ge(scattered[s], 16 * 2 * TPC * (b + (r + 1) // 2))
                    layer_norm_apply(dve, post_norm, [x3[:, i, :] for i in range(TPC)],
                                     [row[:, s, i, 0:D] for i in range(TPC)], 2 * c + 1)

                def router_max(b, r):
                    c = no(b, r)
                    k, uses = post_use(b, r, "LOGITS")
                    dve.wait_ge(filled[k], uses + 1)
                    logits = work[k][:, 0:TPC * E].rearrange("p (i e) -> p i e", e=E)
                    nc.vector.tensor_reduce(col[:, 0, :], logits, AX_X, ALU.max).then_inc(soft_step, 1)
                    dve.wait_ge(soft_step, 2 * c + 1)
                    nc.vector.tensor_tensor(prob[:, 0, :, :], logits,
                                            col[:, 0, :].unsqueeze(2).broadcast_to([P, TPC, E]),
                                            ALU.subtract).then_inc(soft_step, 1)
                    dve.wait_ge(soft_step, 2 * c + 2)
                    settle(dve, freed[k])

                def choose(b, r):
                    c, s = no(b, r), r % 2
                    t = top_step
                    dve.wait_ge(prob_exp, c + 1)
                    nc.vector.tensor_reduce(col[:, 1, :], prob[:, 1, :, :], AX_X, ALU.add).then_inc(t, 1)
                    dve.wait_ge(t, 8 * c + 1)
                    nc.vector.reciprocal(col[:, 2, :], col[:, 1, :]).then_inc(t, 1)
                    dve.wait_ge(t, 8 * c + 2)
                    nc.vector.tensor_tensor(prob[:, 2, :, :], prob[:, 1, :, :],
                                            col[:, 2, :].unsqueeze(2).broadcast_to([P, TPC, E]),
                                            ALU.mult).then_inc(t, 1)
                    dve.wait_ge(t, 8 * c + 3)
                    settle(dve, passed)
                    for i in range(TPC):
                        last = nc.vector.max(top[:, i, :], prob[:, 2, i, :])
                    last.then_inc(t, 1)
                    dve.wait_ge(t, 8 * c + 4)
                    settle(dve, passed)
                    for i in range(TPC):
                        last = nc.vector.max_index(top_i[:, i, :], top[:, i, :], prob[:, 2, i, :])
                    last.then_inc(t, 1)
                    nc.vector.tensor_tensor(col[:, 0, :], top[:, :, 0], top[:, :, 1], ALU.add).then_inc(t, 1)
                    dve.wait_ge(t, 8 * c + 6)
                    nc.vector.reciprocal(col[:, 1, :], col[:, 0, :]).then_inc(t, 1)
                    nc.vector.tensor_copy(row[:, s, :, ROW_E:ROW_E + 2], top_i[:, :, 0:2])
                    nc.vector.tensor_copy(row[:, s, :, ROW_ID:ROW_ID + 1].bitcast(I32),
                                          token_no[:, bass.ds(c * TPC, TPC)].unsqueeze(2)).then_inc(t, 1)
                    dve.wait_ge(t, 8 * c + 8)
                    nc.vector.tensor_tensor(row[:, s, :, ROW_W:ROW_W + 2], top[:, :, 0:2],
                                            col[:, 1, :].unsqueeze(2).broadcast_to([P, TPC, 2]), ALU.mult)
                    for choice in range(2):
                        no_ = expert_no[:, :].unsqueeze(1).broadcast_to([P, TPC, E])
                        last = nc.vector.tensor_tensor(
                            pick[:, choice, :, :], no_,
                            row[:, s, :, ROW_E + choice:ROW_E + choice + 1].broadcast_to([P, TPC, E]), ALU.is_equal)
                    last.then_inc(pick_step, 1)
                    dve.wait_ge(pick_step, c + 1)
                    nc.vector.tensor_tensor(pick[:, 2, :, :], pick[:, 0, :, :], pick[:, 1, :, :], ALU.add)\
                        .then_inc(picked, 1)

                def find_slots(b, r):
                    c, s = no(b, r), r % 2
                    k, uses = post_use(b, r, "RANKS")
                    dve.wait_ge(filled[k], uses + 1)
                    for i in range(TPC):
                        g = c * TPC + i
                        run_now, run_next = (run[:, bass.ds(g + x, 1), :].rearrange("p a e -> p (a e)")
                                             for x in range(2))
                        nc.vector.tensor_tensor(run_next, run_now, work[k][:, (TPC + i) * E:(TPC + i + 1) * E],
                                                ALU.add).then_inc(rank_step, 1)
                        dve.wait_ge(rank_step, 6 * c + i + 1)
                    nc.vector.tensor_tensor(place[:, :, :], run[:, bass.ds(c * TPC, TPC), :],
                                            work[k][:, 0:TPC * E].rearrange("p (i e) -> p i e", e=E),
                                            ALU.add).then_inc(rank_step, 1)
                    dve.wait_ge(rank_step, 6 * c + 5)
                    settle(dve, freed[k])
                    nc.vector.tensor_tensor(placed[:, :, :, :], pick[:, 0:2, :, :],
                                            place[:, :, :].unsqueeze(1).broadcast_to([P, 2, TPC, E]), ALU.mult)\
                        .then_inc(rank_step, 1)
                    dve.wait_ge(rank_step, 6 * c + 6)
                    nc.vector.tensor_reduce(slot_f[:, :, :], placed[:, :, :, :], AX_X, ALU.add).then_inc(slot_step, 1)
                    dve.wait_ge(slot_step, c + 1)
                    nc.vector.tensor_copy(slot[:, s, :, :], slot_f[:, :, :]).then_inc(slots_ready, 1)

                def gate(b, r):
                    c = no(b, r)
                    dve.wait_ge(hc_added, (c + 1) * N + HS)
                    dve.wait_ge(silu_done, 2 * c + (2 if isinstance(c, int) and c == NCH - 1 else 3))
                    nc.vector.tensor_tensor(yg[:, :, :], y_ps[:, :, :], gres[:, r % 2, :, :], ALU.mult)\
                        .then_inc(gated, 1)

                def add_out(b, r, pair):
                    k, uses = post_use(b, r, f"OUT{pair}")
                    dve.wait_ge(filled[k], uses + 1)
                    h = h_all[:, bass.ds(no(b, r) * TPC + 2 * pair, 2), :]
                    nc.vector.tensor_tensor(h, h, work[k][:, 0:2 * D].rearrange("p (a d) -> p a d", a=2),
                                            ALU.add).then_inc(freed[k], 1)

                def scan_chunk(b, r, first=False, last=False):
                    c, s = no(b, r), r % 2
                    dve.wait_ge(du_ready, c + 1)
                    if s == 1:
                        dve.wait_ge(last_saved, (b + 1) * N + 2)
                    for n in range(N):
                        q = c * N + n
                        dve.wait_ge(b_bc_ready, q + 1)
                        dve.wait_ge(scanned, q * MT + 1)
                        nc.vector.tensor_tensor(
                            dbu[:, n % 2, :, :], du[:, s, :, :],
                            b_bc[:, :].rearrange("p (a t) -> p a t", a=1).broadcast_to([P, MT, CH]),
                            ALU.mult).then_inc(dbu_ready, 1)
                        dve.wait_ge(dbu_ready, q + 2)
                        dve.wait_ge(hc_ready, q + 1)
                        if s == 0:
                            dve.wait_ge(last_saved, (b + r // 2) * N + n + 1)
                        for m in range(MT):
                            dve.wait_ge(decay_ready, q * MT + m + 1)
                            init = 0.0 if s == 0 else h_last[:, m, n:n + 1]
                            nc.vector.tensor_tensor_scan(hst[:, n % 2, m, :], decay[:, (n * MT + m) % 2, :],
                                                         dbu[:, n % 2, m, :], init, ALU.mult, ALU.add)\
                                .then_inc(scanned, 1)
                        if not first and n == 1:
                            gate(b, r - 1)
                        if not first and n in (3, 4):
                            add_out(b, r - 1, n - 3)
                        if not first:
                            if n == 4:
                                post_norm_first(b, r - 1)
                            if n == 5:
                                post_norm_mid(b, r - 1)
                            if n == 6:
                                post_norm_last(b, r - 1)
                            if n == 9:
                                router_max(b, r - 1)
                            if n == 12:
                                choose(b, r - 1)
                            if n == 14:
                                find_slots(b, r - 1)
                        if last:
                            continue
                        if n == 5:
                            norm_stats(b, r + 2, 0)
                        if n == 7:
                            norm_apply(b, r + 2, 0)
                            norm_stats(b, r + 2, 1)
                        if n == 10:
                            norm_apply(b, r + 2, 1)
                        if n == 10:
                            next_halo(b, r + 2)
                        if n == 12:
                            split_b(b, r + 1)
                        if n == 13:
                            softplus_abs(b, r + 1)
                        if n == 14:
                            softplus_mid(b, r + 1)
                    if not last:
                        softplus_end(b, r + 1)

                for k in range(2):
                    dve.wait_ge(gathered[k], 16 * TPC)
                    for step in range(2):
                        norm_stats(0, k, step)
                        norm_apply(0, k, step)
                    if k == 0:
                        dve.wait_ge(weights_in, 16 * 11)
                next_halo(0, 1)
                split_b(0, 0)
                softplus_abs(0, 0)
                softplus_mid(0, 0)
                softplus_end(0, 0)
                dve.wait_ge(gathered[2], 16 * (GT - 2 * TPC))
                scan_chunk(0, 0, first=True)
                with dve.Fori(0, BATCH - 1) as b:
                    scan_chunk(b, 1)
                    scan_chunk(b, 2)
                scan_chunk(BATCH - 1, 1, last=True)
                gate(BATCH - 1, 1)
                for pair in range(TPC // 2):
                    add_out(BATCH - 1, 1, pair)
                post_norm_first(BATCH - 1, 1)
                post_norm_mid(BATCH - 1, 1)
                post_norm_last(BATCH - 1, 1)
                router_max(BATCH - 1, 1)
                choose(BATCH - 1, 1)
                find_slots(BATCH - 1, 1)

                steps = [0]

                def step(instruction):
                    steps[0] += 1
                    instruction.then_inc(table_step, 1)
                    dve.wait_ge(table_step, steps[0])

                end = run[:, GT, :]
                step(nc.vector.tensor_tensor(count[:, :], end, list_start[:, :], ALU.subtract))
                step(nc.vector.tensor_tensor(
                    fills[:, :, :], count[:, :].unsqueeze(2).broadcast_to([P, E, TOK // TS]),
                    tile_no[:, 0:TOK // TS].unsqueeze(1).broadcast_to([P, E, TOK // TS]), ALU.is_gt))
                step(nc.vector.tensor_reduce(tiles_of[:, :], fills[:, :, :], AX_X, ALU.add))
                step(nc.vector.tensor_tensor_scan(tile_end[:, :], ones[:, 0:E], tiles_of[:, :], 0.0, ALU.mult, ALU.add))
                step(nc.vector.tensor_tensor(tiles_of[:, :], tile_end[:, :], tiles_of[:, :], ALU.subtract))
                step(nc.vector.scalar_tensor_tensor(tiles_of[:, :], tiles_of[:, :], -float(TS), list_start[:, :],
                                                    ALU.mult, ALU.add))
                step(nc.vector.scalar_tensor_tensor(
                    fit[:, :, :], tile_no[:, :].unsqueeze(2).broadcast_to([P, NT, E]), 1.0 / TS,
                    tile_end[:, :].unsqueeze(1).broadcast_to([P, NT, E]), ALU.mult, ALU.is_ge))
                step(nc.vector.tensor_reduce(te_f[:, :], fit[:, :, :], AX_X, ALU.add))
                step(nc.vector.tensor_scalar(te_i[:, :], te_f[:, :], float(E - 1), None, ALU.min))
                step(nc.vector.tensor_tensor(fit[:, :, :], te_f[:, :].unsqueeze(2).broadcast_to([P, NT, E]),
                                             expert_no[:, :].unsqueeze(1).broadcast_to([P, NT, E]), ALU.is_equal))
                step(nc.vector.tensor_tensor(fit[:, :, :], fit[:, :, :],
                                             tiles_of[:, :].unsqueeze(1).broadcast_to([P, NT, E]), ALU.mult))
                step(nc.vector.tensor_reduce(row_f[:, :], fit[:, :, :], AX_X, ALU.add))
                step(nc.vector.tensor_scalar(idle[:, :], te_f[:, :], float(E), None, ALU.is_lt))
                step(nc.vector.tensor_tensor(idle[:, :], idle[:, :], tile_no[:, :], ALU.mult))
                step(nc.vector.tensor_tensor(row_f[:, :], row_f[:, :], idle[:, :], ALU.add))
                step(nc.vector.tensor_scalar(idle[:, :], te_f[:, :], float(E), float(PAD_ROW), ALU.is_ge, ALU.mult))
                step(nc.vector.tensor_tensor(row_i[:, :], row_f[:, :], idle[:, :], ALU.add))
                nc.vector.tensor_copy(count_i[:, :], end).then_inc(table_ready, 1)

        with ExitStack() as fctx:
            xt = sb("xt", [P, 4, TT, ROW], F32, fctx)
            xt_a = sb("xt_a", [P, 2, TS], F32, fctx)
            xt_b = sb("xt_b", [DH, 2, TS], F32, fctx)
            w1_a = sb("w1_a", [P, 2, DFF], F32, fctx)
            w1_b = sb("w1_b", [DH, 2, DFF], F32, fctx)
            w2_sb = sb("w2_sb", [P, 2, FT, D], F32, fctx)
            hid = sb("hid", [P, 2, FT, TS], F32, fctx)
            share = sb("share", [P, 2, TT, 2], F32, fctx)
            gate_c = sb("gate_c", [P, 2, TT], F32, fctx)
            ys = sb("ys", [P, 2, TT, D], F32, fctx)

            tr = [ps(f"tr{k}", [P, 2 * TS], fctx) for k in range(2)]
            hp = [ps(f"hp{k}", [P, 2 * TS], fctx) for k in range(2)]
            yp = [ps(f"yp{k}", [P, 2 * TS], fctx) for k in range(2)]

            xt_in = [sem(f"xt_in{k}") for k in range(4)]
            w1_in = [sem(f"w1_in{k}") for k in range(2)]
            w2_in = [sem(f"w2_in{k}") for k in range(2)]
            turned = sem("turned")
            xt_moved = sem("xt_moved")
            hid_filled = sem("hid_filled")
            hid_silu = sem("hid_silu")
            y_filled = sem("y_filled")
            share_done = sem("share_done")
            gate_done = sem("gate_done")
            y_gated = sem("y_gated")
            y_sent = sem("y_sent")

            FP = FT // 2
            block2 = fctx.enter_context(nc.Block())

            @block2.sync
            def _(sp):
                def load_rows(q, i):
                    j = q * 4 + i
                    start = sp.value_load(row_i[0:1, bass.ds(j, 1)], min_val=0, max_val=PAD_ROW)
                    sp.dma_start(xt[:, i % 4, :, :], lists[bass.ds(start, TS), :].rearrange("(i p) d -> p i d", p=P))\
                        .then_inc(xt_in[i % 4], 16)

                def load_w1(q, i):
                    j = q * 4 + i
                    e = sp.value_load(te_i[0:1, bass.ds(j, 1)], min_val=0, max_val=E - 1)
                    e_ = bass.ds(e, 1)
                    sp.dma_start(w1_a[:, i % 2:i % 2 + 1, :], w1[e_, 0:P, :].rearrange("e d f -> d e f"))\
                        .then_inc(w1_in[i % 2], 16)
                    sp.dma_start(w1_b[:, i % 2:i % 2 + 1, :], w1[e_, P:D, :].rearrange("e d f -> d e f"))\
                        .then_inc(w1_in[i % 2], 16)

                def load_w2(q, i):
                    j = q * 4 + i
                    e = sp.value_load(te_i[0:1, bass.ds(j, 1)], min_val=0, max_val=E - 1)
                    sp.dma_start(w2_sb[:, i % 2, :, :],
                                 w2[bass.ds(e, 1), :, :].rearrange("e (f p) d -> p (e f) d", p=P))\
                        .then_inc(w2_in[i % 2], 16)

                for j in range(2):
                    load_rows(0, j)
                    load_w1(0, j)
                    load_w2(0, j)
                load_rows(0, 2)
                load_rows(0, 3)

                def ahead(q, i, last=False):
                    j = q * 4 + i
                    if not (last and i >= 2):
                        sp.wait_ge(hid_filled, (j + 1) * FP)
                        settle(sp, passed)
                        load_w1(q, i + 2)
                        sp.wait_ge(y_filled, j + 3)
                        settle(sp, passed)
                        load_w2(q, i + 2)
                    if not last:
                        sp.wait_ge(y_sent, (j + 1) * TT * 16)
                        settle(sp, passed)
                        load_rows(q + 1, i)

                with sp.Fori(0, NT // 4 - 1) as q:
                    for i in range(4):
                        ahead(q, i)
                for i in range(4):
                    ahead(NT // 4 - 1, i, last=True)

            @block2.gpsimd
            def _(pool):
                def send(q, i):
                    j = q * 4 + i
                    for t in range(TT):
                        pool.wait_ge(y_gated, (j * TT) + t + 3)
                        if not (isinstance(j, int) and j * TT + t == 0):
                            pool.wait_ge(y_sent, (j * TT + t) * 16)
                        settle(pool, passed)
                        nc.gpsimd.indirect_dma_start(
                            out, bass.IndirectOffsetOnAxis(xt[:, i, t, ROW_ID:ROW_ID + 1].bitcast(U32), 0),
                            ys[:, i % 2, t, :], None, bounds_check=TOK - 1, oob_is_err=False,
                            compute_op=ALU.add).then_inc(y_sent, 16)

                for i in range(4):
                    send(0, i)
                with pool.Fori(1, NT // 4) as q:
                    for i in range(4):
                        send(q, i)
                pool.wait_ge(y_sent, NT * TT * 16)

            @block2.scalar
            def _(act):
                def move(q, i):
                    j = q * 4 + i
                    act.wait_ge(turned, j + 1)
                    if not (isinstance(j, int) and j < 2):
                        act.wait_ge(hid_filled, (j - 1) * FP)
                    nc.scalar.activation(xt_a[:, i % 2, :], tr[i % 2][:, 0:TS], ACT.Identity,
                                         scale=gamma[0], bias=beta[0])
                    nc.scalar.activation(xt_b[:, i % 2, :], tr[i % 2][0:DH, TS:2 * TS], ACT.Identity,
                                         scale=gamma[1], bias=beta[1]).then_inc(xt_moved, 1)

                def silu(q, i):
                    j = q * 4 + i
                    act.wait_ge(y_filled, j + 1)
                    for f in range(FP):
                        act.wait_ge(hid_filled, j * FP + f + 1)
                        nc.scalar.activation(hid[:, i % 2, 2 * f:2 * f + 2, :], hp[(i * FP + f) % 2][:, :], ACT.Silu)\
                            .then_inc(hid_silu, 1)

                move(0, 0)
                move(0, 1)
                silu(0, 0)
                move(0, 2)
                silu(0, 1)
                with act.Fori(0, NT // 4 - 1) as q:
                    for i in range(4):
                        move(q, i + 3) if i == 0 else move(q + 1, i - 1)
                        silu(q, i + 2) if i < 2 else silu(q + 1, i - 2)
                move(NT // 4 - 1, 3)
                silu(NT // 4 - 1, 2)
                silu(NT // 4 - 1, 3)

            @block2.tensor
            def _(pe):
                def turn(q, i):
                    j = q * 4 + i
                    pe.wait_ge(xt_in[i], q * 16 + 16)
                    pe.wait_ge(xt_moved, j + 1)
                    settle(pe, passed)
                    for t in range(TT):
                        nc.tensor.transpose(tr[i % 2][:, t * P:(t + 1) * P], xt[:, i, t, 0:P], ident[:, :])
                        mm = nc.tensor.transpose(tr[i % 2][0:DH, TS + t * P:TS + (t + 1) * P], xt[:, i, t, P:D],
                                                 ident[:, :])
                    mm.then_inc(turned, 1)

                def first_product(q, i):
                    j = q * 4 + i
                    pe.wait_ge(xt_moved, j + 3)
                    pe.wait_ge(w1_in[i % 2], (q * 2 + i // 2 + 1) * 32)
                    for f in range(FT):
                        if f % 2 == 0:
                            pe.wait_ge(hid_silu, j * FP + f // 2 + 1)
                        h = hp[(i * FP + f // 2) % 2][:, (f % 2) * TS:(f % 2 + 1) * TS]
                        nc.tensor.matmul(h, w1_a[:, i % 2, f * P:(f + 1) * P], xt_a[:, i % 2, :],
                                         start=True, stop=False)
                        mm = nc.tensor.matmul(h, w1_b[:, i % 2, f * P:(f + 1) * P], xt_b[:, i % 2, :],
                                              start=False, stop=True)
                        if f % 2:
                            mm.then_inc(hid_filled, 1)

                def second_product(q, i):
                    j = q * 4 + i
                    pe.wait_ge(w2_in[i % 2], (q * 2 + i // 2 + 1) * 16)
                    pe.wait_ge(hid_silu, (j + 1) * FP + 2)
                    pe.wait_ge(y_gated, j * TT + 1)
                    for t in range(TT):
                        for f in range(FT):
                            mm = nc.tensor.matmul(yp[i % 2][:, t * D:(t + 1) * D], hid[:, i % 2, f, t * P:(t + 1) * P],
                                                  w2_sb[:, i % 2, f, :], start=(f == 0), stop=(f == FT - 1))
                    mm.then_inc(y_filled, 1)

                def at_tile(stage, q, i):
                    stage(q, i) if i < 4 else stage(q + 1, i - 4)

                turn(0, 0)
                turn(0, 1)
                first_product(0, 0)
                with pe.Fori(0, NT // 4 - 1) as q:
                    for i in range(4):
                        at_tile(turn, q, i + 2)
                        at_tile(first_product, q, i + 1)
                        second_product(q, i)
                q = NT // 4 - 1
                for i in range(4):
                    if i < 2:
                        turn(q, i + 2)
                    if i < 3:
                        first_product(q, i + 1)
                    second_product(q, i)

            @block2.vector
            def _(dve):
                for reads in (xt_moved, hid_silu, y_filled, y_gated):
                    nc.vector.sem_inc(reads, 2)

                def weigh(q, i):
                    j = q * 4 + i
                    dve.wait_ge(xt_in[i], q * 16 + 16)
                    nc.vector.scalar_tensor_tensor(share[:, i % 2, :, :], xt[:, i, :, ROW_E:ROW_E + 2],
                                                   te_f[:, bass.ds(j, 1)], xt[:, i, :, ROW_W:ROW_W + 2],
                                                   ALU.is_equal, ALU.mult).then_inc(share_done, 1)
                    dve.wait_ge(share_done, j + 1)
                    nc.vector.tensor_reduce(gate_c[:, i % 2, :], share[:, i % 2, :, :], AX_X, ALU.add)\
                        .then_inc(gate_done, 1)
                    dve.wait_ge(gate_done, j + 1)
                    dve.wait_ge(y_filled, j + 3)
                    if not (isinstance(j, int) and j < 2):
                        dve.wait_ge(y_sent, (j - 1) * TT * 16)
                    for t in range(TT):
                        nc.vector.tensor_scalar(ys[:, i % 2, t, :], yp[i % 2][:, t * D:(t + 1) * D],
                                                gate_c[:, i % 2, t:t + 1], None, ALU.mult).then_inc(y_gated, 1)

                for i in range(4):
                    weigh(0, i)
                with dve.Fori(1, NT // 4) as q:
                    for i in range(4):
                        weigh(q, i)


def kernel(**inputs):
    import ml_dtypes
    import concourse.bacc as bacc
    from concourse.bass_utils import run_bass_kernel_spmd

    a = {k: np.asarray(v) for k, v in inputs.items()}

    def tiles(x, fill=P):
        x = x.reshape(x.shape[0], -1)
        return x.reshape(-1, P, x.shape[1]).transpose(1, 0, 2).reshape(P, -1)

    def halves(x):
        v = np.zeros((P, 2), np.float32)
        v[:, 0] = x[:P]
        v[:DH, 1] = x[P:]
        return v

    c128 = np.concatenate(
        [halves(a["L0_attn_ln_w"]), halves(a["L0_attn_ln_b"]), halves(a["L0_ffn_ln_gamma"]),
         halves(a["L0_ffn_ln_beta"]), np.zeros((P, 3), np.float32), tiles(a["L0_attn_conv_w"][:, 0, :]),
         tiles(a["L0_attn_conv_b"]), tiles(a["L0_attn_dt_proj_b"]), tiles(a["L0_attn_D_param"]),
         tiles(a["L0_attn_A_log"])], axis=1)
    xp = a["L0_attn_x_proj_w"].T
    w_x = np.zeros((DI, XR), np.float32)
    w_x[:, DT0:DT0 + R] = xp[:, 0:R]
    w_x[:, B0:B0 + N] = xp[:, R:R + N]
    w_x[:, C0:C0 + N] = xp[:, R + N:R + 2 * N]
    sel = np.zeros((96, N, P), ml_dtypes.bfloat16)
    for part in range(3):
        for n in range(N):
            sel[32 * part + n, n, :] = 1
    arrays = {
        "ids": a["x"].reshape(GT, P).T,
        "emb": a["L0_tok_W"],
        "c128": c128,
        "ident_d": np.eye(P, dtype=np.float32),
        "sel_d": sel,
        "before_d": np.triu(np.ones((P, P), np.float32), 1),
        "w_in": a["L0_attn_in_proj_w"].T,
        "w_x": w_x,
        "w_dt": a["L0_attn_dt_proj_w"].T,
        "w_out": a["L0_attn_out_proj_w"].T,
        "router_w": a["L0_ffn_router_w"],
        "w1": a["L0_ffn_w1"],
        "w2": a["L0_ffn_w2"],
    }
    nc = bacc.Bacc("TRN2", target_bir_lowering=False, num_devices=1)
    fed, args = {}, []
    for name, x in arrays.items():
        fed[name] = np.ascontiguousarray(x)
        args.append(nc.dram_tensor(name, x.shape, mybir.dt.from_np(x.dtype), kind="ExternalInput").ap())
    out = nc.dram_tensor("out", (TOK, D), F32, kind="ExternalOutput").ap()
    c_scratch = nc.dram_tensor("c_scratch", (HALVES, N, CH), F32, kind="Internal").ap()
    lists = nc.dram_tensor("lists", ((E * LIST + TS), ROW), F32, kind="Internal").ap()
    mamba_moe(nc, *args, out, c_scratch, lists)
    r = run_bass_kernel_spmd(nc, [fed], core_ids=[0])
    return r.results[0]["out"].reshape(BATCH, SEQ, D)
```

```python
from contextlib import ExitStack

import numpy as np

import concourse.bass as bass
from concourse import mybir

F32 = mybir.dt.float32
BF16 = mybir.dt.bfloat16
U32 = mybir.dt.uint32
I32 = mybir.dt.int32
ALU = mybir.AluOpType
ACT = mybir.ActivationFunctionType
AX_X = mybir.AxisListType.X

P = 128
VOCAB = 8000
D = 192
DH = D - P
DI = 384
MT = DI // P
N = 16
TAPS = 4
R = 48
BATCH, SEQ = 4, 1024
TOK = BATCH * SEQ
CH = 512
TPC = CH // P
HALVES = SEQ // CH
NCH = TOK // CH
GT = TOK // P
DFF, E = 768, 8
FT = DFF // P
EPS = 1e-5
DT0, B0, C0, XR = 0, 64, 96, 112
CG = 2

ROW_ID, ROW_W, ROW_E, ROW = D, D + 1, D + 3, D + 5
TS = 256
TT = TS // P
LIST = TOK + TS
PAD_ROW = E * LIST
NT = 40
assert (2 * TOK + E * (TS - 1)) // TS < NT and NT % 4 == 0
HALO = TAPS - 1
HS = 4
AHEAD = 3
PAST = 0x7FFFFFFF
EXP_LN = "natural_log_exp_and_others"

ORDER = ["pre CONV2", "post OUT0", "post OUT1", "pre RES0", "pre XP", "pre RES1", "pre DT0", "pre DT1",
         "pre DT2", "post TA", "post TB", "pre RES2", "post LOGITS", "early TA", "early TB", "early IN0",
         "early IN1", "early IN2", "post RANKS", "early CONV0", "early CONV1"]
USES = len(ORDER)
EARLY = [x[6:] for x in ORDER if x.startswith("early ")]
PRE = [x[4:] for x in ORDER if x.startswith("pre ")]
POST = [x[5:] for x in ORDER if x.startswith("post ")]
assert len(ORDER) == len(EARLY) + len(PRE) + len(POST)
EMPTY = ("RANKS",)
FIRST_USE = len(POST) - len(EMPTY)
FIRST_SCAN = 2 * len(EARLY) + len(PRE)


def bank_of(b, i):
    return i % 2, b * USES + i // 2


def pre_use(b, r, what):
    k = 2 * b + r if isinstance(b, int) else 2
    if what in EARLY:
        if k == 0:
            return bank_of(0, FIRST_USE + EARLY.index(what))
        if k == 1:
            return bank_of(0, FIRST_USE + len(EARLY) + len(PRE) + EARLY.index(what))
        at = ORDER.index("early " + what)
        return bank_of(b, FIRST_SCAN + (r - 2) * USES + at)
    if k == 0:
        return bank_of(0, FIRST_USE + len(EARLY) + PRE.index(what))
    if k == 1:
        return bank_of(0, FIRST_USE + 2 * len(EARLY) + len(PRE) + PRE.index(what))
    return bank_of(b, FIRST_SCAN + (r - 1) * USES + ORDER.index("pre " + what))


def post_use(b, r, what):
    if isinstance(b, int) and 2 * b + r >= NCH - 2:
        return bank_of(0, FIRST_SCAN + (NCH - 1) * USES + (2 * b + r - NCH + 2) * len(POST) + POST.index(what))
    return bank_of(b, FIRST_SCAN + (r + 1) * USES + ORDER.index("post " + what))


def settle(eng, passed):
    eng.sem_inc(passed, 1)


def mamba_moe(nc, ids, emb, c128, ident_d, sel_d, before_d, w_in, w_x, w_dt, w_out, router_w, w1, w2,
              out, c_scratch, lists):
    with ExitStack() as ctx:
        def sb(name, shape, dt=F32, stack=ctx):
            return stack.enter_context(nc.sbuf_tensor(name, shape, dt))

        def ps(name, shape, stack=ctx):
            return stack.enter_context(nc.psum_tensor(name, shape, F32))

        def sem(name):
            return ctx.enter_context(nc.semaphore(name))

        ids_sb = sb("ids_sb", [P, GT], I32)
        h_all = sb("h_all", [P, GT + TPC, D])
        ident = sb("ident", [P, P])
        minus_half = sb("minus_half", [P, TPC])

        class Norm:

            def __init__(self, name):
                self.stats = sb(f"{name}_stats", [P, TPC, 6])
                self.mv = sb(f"{name}_mv", [P, TPC, 2])
                self.var_eps = sb(f"{name}_var_eps", [P, TPC])
                self.rstd = sb(f"{name}_rstd", [P, TPC])
                self.stats_done = sem(f"{name}_stats_done")
                self.aggr_done = sem(f"{name}_aggr_done")
                self.var_ready = sem(f"{name}_var_ready")
                self.rstd_done = sem(f"{name}_rstd_done")
                self.norm_done = sem(f"{name}_norm_done")

        pre_norm, post_norm = Norm("pre"), Norm("post")
        x1 = sb("x1", [P, TPC, D])
        vec = sb("vec", [P, 8 + MT * (TAPS + 3 + N)])

        te_f = sb("te_f", [P, NT])
        te_i = sb("te_i", [P, NT], I32)
        row_i = sb("row_i", [P, NT], I32)
        count_i = sb("count_i", [P, E], I32)
        pad = sb("pad", [P, TT, ROW])

        ids_in = sem("ids_in")
        pad_ready = sem("pad_ready")
        scattered = [sem(f"scattered{k}") for k in range(2)]
        table_ready = sem("table_ready")
        padded = sem("padded")
        passed = sem("passed")
        weights_in = sem("weights_in")
        h_zero = sem("h_zero")
        half_ready = sem("half_ready")
        pad_zero = sem("pad_zero")
        gathered = [sem(f"gathered{k}") for k in range(3)]

        ln_w, ln_b = (vec[:, 0:1], vec[0:DH, 1:2]), (vec[:, 2:3], vec[0:DH, 3:4])
        gamma, beta = (vec[:, 4:5], vec[0:DH, 5:6]), (vec[:, 6:7], vec[0:DH, 7:8])
        at = 8

        def cols(width):
            nonlocal at
            v = vec[:, at:at + MT * width].rearrange("p (m k) -> p m k", m=MT)
            at += MT * width
            return v

        conv_w, conv_b, dt_b, d_par, a_log = cols(TAPS), cols(1), cols(1), cols(1), cols(N)

        def layer_norm_stats(dve, w, src, k):
            for i in range(TPC):
                last = nc.vector.bn_stats(w.stats[:, i, :], src[i])
            last.then_inc(w.stats_done, 1)
            dve.wait_ge(w.stats_done, k + 1)
            settle(dve, passed)
            for i in range(TPC):
                last = nc.vector.bn_aggr(w.mv[:, i, :], w.stats[:, i, :])
            last.then_inc(w.aggr_done, 1)
            dve.wait_ge(w.aggr_done, k + 1)
            nc.vector.tensor_scalar(w.var_eps[:, :], w.mv[:, :, 1], EPS, None, ALU.add).then_inc(w.var_ready, 1)

        def layer_norm_power(pool, w, k):
            pool.wait_ge(w.var_ready, k + 1)
            nc.gpsimd.tensor_tensor(w.rstd[:, :], w.var_eps[:, :], minus_half[:, :], ALU.pow)\
                .then_inc(w.rstd_done, 1)

        def layer_norm_apply(dve, w, src, dst, k):
            dve.wait_ge(w.rstd_done, k + 1)
            for i in range(TPC):
                last = nc.vector.tensor_scalar(dst[i], src[i], w.mv[:, i, 0:1], w.rstd[:, i:i + 1],
                                               ALU.subtract, ALU.mult)
            last.then_inc(w.norm_done, 1)
            dve.wait_ge(w.norm_done, k + 1)

        with ExitStack() as mctx:
            w_in_a = sb("w_in_a", [P, 2 * DI], F32, mctx)
            w_in_b = sb("w_in_b", [DH, 2 * DI], F32, mctx)
            w_x_sb = sb("w_x_sb", [P, MT, XR], F32, mctx)
            w_dt_sb = sb("w_dt_sb", [R, DI], F32, mctx)
            w_out_sb = sb("w_out_sb", [P, MT, D], F32, mctx)
            sel = sb("sel", [96, N, P], BF16, mctx)
            a_neg = sb("a_neg", [P, MT, N], F32, mctx)
            a_exp = sb("a_exp", [P, MT, N], F32, mctx)
            conv_diag = sb("conv_diag", [P, MT, TAPS, P], F32, mctx)
            d_diag = sb("d_diag", [P, MT, P], F32, mctx)
            xn_a = sb("xn_a", [P, CH], F32, mctx)
            xn_b = sb("xn_b", [DH, CH], F32, mctx)
            xin = sb("xin", [P, MT, HALO + CH], F32, mctx)
            gres = sb("gres", [P, 2, MT, CH], F32, mctx)
            u_sb = sb("u_sb", [P, 2, MT, CH], F32, mctx)
            dt_sb = sb("dt_sb", [R, CH], F32, mctx)
            bc_rows = sb("bc_rows", [32 + N, CH], F32, mctx)
            b_rows, c_rows = bc_rows[0:N, :], bc_rows[32:32 + N, :]
            b_part = sb("b_part", [N, CH], BF16, mctx)
            b_parts = sb("b_parts", [96, 2, CH], BF16, mctx)
            sp_one = sb("sp_one", [P, MT, CH], F32, mctx)
            delta = sb("delta", [P, 2, MT, CH], F32, mctx)
            du = sb("du", [P, 2, MT, CH], F32, mctx)
            c_bc = sb("c_bc", [P, 2, CG, CH], F32, mctx)
            dbu = sb("dbu", [P, 2, MT, CH], F32, mctx)
            hst = sb("hst", [P, 2, MT, CH], F32, mctx)
            hc = sb("hc", [P, HS, MT, CH], F32, mctx)
            h_last = sb("h_last", [P, MT, N], F32, mctx)
            yg = sp_one

            before = sb("before", [P, P], F32, mctx)
            ones = sb("ones", [P, P], F32, mctx)
            router_a = sb("router_a", [P, E], F32, mctx)
            router_b = sb("router_b", [DH, E], F32, mctx)
            expert_no = sb("expert_no", [P, E], F32, mctx)
            list_start = sb("list_start", [P, E], F32, mctx)
            token_no = sb("token_no", [P, GT], I32, mctx)
            x3 = sb("x3", [P, TPC, D], F32, mctx)
            row = sb("row", [P, 2, TPC, ROW], F32, mctx)
            xm_a = sb("xm_a", [P, CH], F32, mctx)
            xm_b = sb("xm_b", [DH, CH], F32, mctx)
            col = sb("col", [P, 4, TPC], F32, mctx)
            prob = sb("prob", [P, 3, TPC, E], F32, mctx)
            top = sb("top", [P, TPC, 8], F32, mctx)
            top_i = sb("top_i", [P, TPC, 8], U32, mctx)
            pick = sb("pick", [P, 3, TPC, E], F32, mctx)
            place = sb("place", [P, TPC, E], F32, mctx)
            placed = sb("placed", [P, 2, TPC, E], F32, mctx)
            slot_f = sb("slot_f", [P, 2, TPC], F32, mctx)
            slot = sb("slot", [P, 2, 2, TPC], U32, mctx)
            tile_no = sb("tile_no", [P, NT], F32, mctx)
            count = sb("count", [P, E], F32, mctx)
            fills = sb("fills", [P, E, TOK // TS], F32, mctx)
            tiles_of = sb("tiles_of", [P, E], F32, mctx)
            tile_end = sb("tile_end", [P, E], F32, mctx)
            fit = sb("fit", [P, NT, E], F32, mctx)
            row_f = sb("row_f", [P, NT], F32, mctx)
            idle = sb("idle", [P, NT], F32, mctx)
            run = sb("run", [P, GT + 1, E], F32, mctx)

            work = [ps(f"work{k}", [P, CH], mctx) for k in range(2)]
            b_bc = ps("b_bc", [P, CH], mctx)
            decay_ps = ps("decay_ps", [P, 2, CH], mctx)
            decay_sb = sb("decay_sb", [P, CH], F32, mctx)
            decay = [decay_ps[:, 0, :], decay_ps[:, 1, :], decay_sb[:, :]]
            y_ps = ps("y_ps", [P, MT, CH], mctx)

            filled = [sem(f"work_filled{k}") for k in range(2)]
            freed = [sem(f"work_freed{k}") for k in range(2)]
            diag_ready = sem("diag_ready")
            a_exp_done = sem("a_exp_done")
            a_ready = sem("a_ready")
            halo_ready = sem("halo_ready")
            silu_done = sem("silu_done")
            rows_ready = sem("rows_ready")
            split_step = sem("split_step")
            parts_ready = sem("parts_ready")
            c_stored = sem("c_stored")
            c_loaded = [sem(f"c_loaded{k}") for k in range(2)]
            abs_done = sem("abs_done")
            exp_done = sem("exp_done")
            one_done = sem("one_done")
            ln_done = sem("ln_done")
            sp_step = sem("sp_step")
            delta_ready = sem("delta_ready")
            du_ready = sem("du_ready")
            b_bc_ready = sem("b_bc_ready")
            dbu_ready = sem("dbu_ready")
            decay_ready = sem("decay_ready")
            scanned = sem("scanned")
            last_saved = sem("last_saved")
            hc_ready = sem("hc_ready")
            hc_added = sem("hc_added")
            gated = sem("gated")
            iota_ready = sem("iota_ready")
            run_begun = sem("run_begun")
            residual_added = sem("residual_added")
            stored = sem("stored")
            soft_step = sem("soft_step")
            prob_exp = sem("prob_exp")
            top_step = sem("top_step")
            pick_step = sem("pick_step")
            picked = sem("picked")
            slot_step = sem("slot_step")
            rank_step = sem("rank_step")
            slots_ready = sem("slots_ready")
            table_step = sem("table_step")

            block = mctx.enter_context(nc.Block())

            def no(b, r):
                return b * 2 + r

            def pad_list(eng, e):
                end = eng.value_load(count_i[0:1, e:e + 1], min_val=e * LIST, max_val=e * LIST + TOK)
                eng.dma_start(lists[bass.ds(end, TS), :].rearrange("(i p) d -> p i d", p=P), pad[:, :, :])\
                    .then_inc(padded, 16)

            @block.sync
            def _(sp):
                sp.dma_start(ids_sb[:, :], ids).then_inc(ids_in, 16)
                for dst, src in ((vec[:, :], c128), (ident[:, :], ident_d), (sel[:, :, :], sel_d),
                                 (w_in_a[:, :], w_in[0:P, :]), (w_in_b[:, :], w_in[P:D, :]),
                                 (w_x_sb[:, :, :], w_x.rearrange("(m p) r -> p m r", p=P)),
                                 (w_dt_sb[:, :], w_dt), (before[:, :], before_d),
                                 (router_a[:, :], router_w[0:P, :]), (router_b[:, :], router_w[P:D, :]),
                                 (w_out_sb[:, :, :], w_out.rearrange("(m p) r -> p m r", p=P))):
                    sp.dma_start(dst, src).then_inc(weights_in, 16)

                def spread_c(b, r, first=False):
                    c, s = no(b, r), r % 2
                    sp.wait_ge(rows_ready, 2 * c + 2)
                    sp.dma_start(c_scratch[s], c_rows[:, :]).then_inc(c_stored, 16)
                    sp.wait_ge(c_stored, 16 * c + 16)
                    settle(sp, passed)
                    for g in range(N // CG):
                        if not (first and g < 2):
                            sp.wait_ge(hc_ready, c * N + (g - 1) * CG + 2)
                            settle(sp, passed)
                        src = c_scratch[s:s + 1, g * CG:(g + 1) * CG, :].broadcast_to([P, CG, CH])
                        sp.dma_start(c_bc[:, g % 2, :, :], src).then_inc(c_loaded[g % 2], 16)

                def store_residual(b, r):
                    c = no(b, r)
                    sp.wait_ge(residual_added, c + 1)
                    settle(sp, passed)
                    src = h_all[:, bass.ds(c * TPC, TPC), :]
                    sp.dma_start(out[bass.ds(c * CH, CH), :].rearrange("(g p) d -> p g d", p=P), src)\
                        .then_inc(stored, 16)

                spread_c(0, 0, first=True)
                with sp.Fori(0, BATCH - 1) as b:
                    spread_c(b, 1)
                    store_residual(b, 0)
                    spread_c(b, 2)
                    store_residual(b, 1)
                spread_c(BATCH - 1, 1)
                store_residual(BATCH - 1, 0)
                store_residual(BATCH - 1, 1)
                sp.wait_ge(stored, 16 * NCH)
                sp.wait_ge(pad_ready, 1)
                sp.dma_start(lists[PAD_ROW:PAD_ROW + TS, :].rearrange("(i p) d -> p i d", p=P), pad[:, :, :])\
                    .then_inc(padded, 16)
                sp.wait_ge(table_ready, 1)
                for e in range(E // 2):
                    pad_list(sp, e)
                sp.wait_ge(padded, 16 * (E + 1))

            @block.gpsimd
            def _(pool):
                nc.gpsimd.memset(minus_half[:, :], -0.5).then_inc(half_ready, 1)
                nc.gpsimd.iota(expert_no[:, :], [[1, E]], base=0, channel_multiplier=0,
                               allow_small_or_imprecise_dtypes=True)
                nc.gpsimd.iota(list_start[:, :], [[LIST, E]], base=0, channel_multiplier=0,
                               allow_small_or_imprecise_dtypes=True)
                nc.gpsimd.iota(tile_no[:, :], [[TS, NT]], base=0, channel_multiplier=0,
                               allow_small_or_imprecise_dtypes=True)
                nc.gpsimd.iota(token_no[:, :], [[P, GT]], base=0, channel_multiplier=1).then_inc(iota_ready, 1)
                nc.gpsimd.memset(pad[:, :, :], 0.0).then_inc(pad_zero, 1)
                pool.wait_ge(pad_zero, 1)
                nc.gpsimd.iota(pad[:, :, ROW_ID:ROW_ID + 1].bitcast(I32), [[0, TT]], base=TOK, channel_multiplier=0)\
                    .then_inc(pad_ready, 1)
                pool.wait_ge(ids_in, 16)
                for g in range(GT):
                    if g in (0, TPC):
                        pool.wait_ge(h_zero, 1 if g == 0 else 2)
                    if g == 2 * TPC:
                        pool.wait_ge(half_ready, 1)
                    if g >= 2 * TPC and g % 2 == 0 and (g - 2 * TPC) // 2 < 4:
                        layer_norm_power(pool, pre_norm, (g - 2 * TPC) // 2)
                    nc.gpsimd.indirect_dma_start(
                        h_all[:, g, :], None, emb, bass.IndirectOffsetOnAxis(ids_sb[:, g:g + 1].bitcast(U32), 0),
                        bounds_check=VOCAB - 1, oob_is_err=False).then_inc(gathered[min(g // TPC, 2)], 16)

                def delta_u(b, r):
                    c, s = no(b, r), r % 2
                    pool.wait_ge(silu_done, 2 * c + 1)
                    pool.wait_ge(delta_ready, c + 1)
                    nc.gpsimd.tensor_tensor(du[:, s, :, :], delta[:, s, :, :], u_sb[:, s, :, :], ALU.mult)\
                        .then_inc(du_ready, 1)

                def scatter(b, r, k):
                    s, choice, i = r % 2, k // TPC, k % TPC
                    nc.gpsimd.indirect_dma_start(
                        lists, bass.IndirectOffsetOnAxis(slot[:, s, choice, i:i + 1], 0), row[:, s, i, :], None,
                        bounds_check=E * LIST - 1, oob_is_err=False).then_inc(scattered[s], 16)

                def scan_chunk(b, r, first=False, last=False):
                    c, s = no(b, r), r % 2
                    for n in range(N):
                        q = c * N + n
                        if n == 0 and not first:
                            pool.wait_ge(slots_ready, c)
                        if n % CG == 0:
                            g = n // CG
                            pool.wait_ge(c_loaded[g % 2], 16 * (N // CG // 2 * c + g // 2 + 1))
                            settle(pool, passed)
                        pool.wait_ge(scanned, MT * (q + 2))
                        if s == 0:
                            settle(pool, passed)
                            nc.gpsimd.tensor_copy(h_last[:, :, n:n + 1], hst[:, n % 2, :, CH - 1:CH])\
                                .then_inc(last_saved, 1)
                        pool.wait_ge(hc_added, q + 1)
                        nc.gpsimd.tensor_tensor(hc[:, n % HS, :, :], hst[:, n % 2, :, :],
                                                c_bc[:, (n // CG) % 2, n % CG:n % CG + 1, :].broadcast_to([P, MT, CH]),
                                                ALU.mult).then_inc(hc_ready, 1)
                        if not last and n in (2, 3):
                            layer_norm_power(pool, pre_norm, 2 * (c + 2) + (n == 3))
                        if not first and n in (5, 7):
                            layer_norm_power(pool, post_norm, 2 * (c - 1) + (n == 7))
                        if not first and 6 <= n < 14:
                            scatter(b, r - 2, n - 6)
                        if not last and n == 14:
                            delta_u(b, r + 1)

                delta_u(0, 0)
                scan_chunk(0, 0, first=True)
                with pool.Fori(0, BATCH - 1) as b:
                    scan_chunk(b, 1)
                    scan_chunk(b, 2)
                scan_chunk(BATCH - 1, 1, last=True)
                pool.wait_ge(slots_ready, NCH)
                for k in range(2 * TPC):
                    scatter(BATCH - 1, 0, k)
                for step in range(2):
                    layer_norm_power(pool, post_norm, 2 * (NCH - 1) + step)
                pool.wait_ge(slots_ready, NCH + 1)
                for k in range(2 * TPC):
                    scatter(BATCH - 1, 1, k)
                pool.wait_ge(scattered[0], 16 * 2 * TPC * BATCH)
                pool.wait_ge(scattered[1], 16 * 2 * TPC * (BATCH + 1))

            @block.scalar
            def _(act):
                act.wait_ge(weights_in, 16 * 11)
                nc.scalar.preload_act_table_set(EXP_LN)
                nc.scalar.activation(a_exp[:, :, :], a_log, ACT.Exp).then_inc(a_exp_done, 1)
                act.wait_ge(a_exp_done, 1)
                nc.scalar.mul(a_neg[:, :, :], a_exp[:, :, :], -1.0).then_inc(a_ready, 1)
                act.wait_ge(a_ready, 1)

                def evacuate(b, r, u, dst, r0=0, r1=P, **kw):
                    k, uses = pre_use(b, r, u)
                    act.wait_ge(filled[k], uses + 1)
                    func = ACT.Identity if kw else ACT.Copy
                    nc.scalar.activation(dst, work[k][r0:r1, :], func, **kw).then_inc(freed[k], 1)

                def post_norm_out(b, r):
                    for what, dst, r1, part in (("TA", xm_a, P, 0), ("TB", xm_b, DH, 1)):
                        k, uses = post_use(b, r, what)
                        act.wait_ge(filled[k], uses + 1)
                        nc.scalar.activation(dst[:, :], work[k][0:r1, :], ACT.Identity,
                                             scale=gamma[part], bias=beta[part]).then_inc(freed[k], 1)

                def router_exp(b, r):
                    act.wait_ge(soft_step, 2 * no(b, r) + 2)
                    nc.scalar.activation(prob[:, 1, :, :], prob[:, 0, :, :], ACT.Exp).then_inc(prob_exp, 1)

                def norm_out(b, r, part):
                    dst, rows = ((xn_a, P), (xn_b, DH))[part]
                    evacuate(b, r, ("TA", "TB")[part], dst[:, :], 0, rows, scale=ln_w[part], bias=ln_b[part])

                def xin_out(b, r, m):
                    if m == 0:
                        act.wait_ge(halo_ready, no(b, r) + 1)
                    evacuate(b, r, f"IN{m}", xin[:, m, HALO:HALO + CH])

                def gres_out(b, r, m):
                    evacuate(b, r, f"RES{m}", gres[:, r % 2, m, :])

                def conv_out(b, r, m):
                    evacuate(b, r, f"CONV{m}", u_sb[:, r % 2, m, :], bias=conv_b[:, m, :])

                def silus(b, r, gate_chunk):
                    k, uses = pre_use(b, r, "CONV2")
                    act.wait_ge(freed[k], uses + 2)
                    nc.scalar.activation(u_sb[:, r % 2, :, :], u_sb[:, r % 2, :, :], ACT.Silu).then_inc(silu_done, 1)
                    if gate_chunk:
                        nc.scalar.activation(gres[:, 1 - r % 2, :, :], gres[:, 1 - r % 2, :, :], ACT.Silu)\
                            .then_inc(silu_done, 1)
                    nc.scalar.preload_act_table_set(EXP_LN)

                def rows_out(b, r):
                    c = no(b, r)
                    k, uses = pre_use(b, r, "XP")
                    act.wait_ge(filled[k], uses + 1)
                    nc.scalar.activation(b_rows[:, :], work[k][B0:B0 + N, :], ACT.Copy).then_inc(rows_ready, 1)
                    if not (isinstance(c, int) and c == 0):
                        act.wait_ge(c_stored, 16 * c)
                    nc.scalar.activation(c_rows[:, :], work[k][C0:C0 + N, :], ACT.Copy).then_inc(rows_ready, 1)
                    evacuate(b, r, "XP", dt_sb[:, :], DT0, DT0 + R)

                def dt_out(b, r, m):
                    evacuate(b, r, f"DT{m}", delta[:, r % 2, m, :], bias=dt_b[:, m, :])

                def softplus_abs(b, r, m0, m1):
                    for m in range(m0, m1):
                        k, uses = pre_use(b, r, f"DT{m}")
                        act.wait_ge(freed[k], uses + 2)
                    nc.scalar.activation(du[:, r % 2, m0:m1, :], delta[:, r % 2, m0:m1, :], ACT.Abs)\
                        .then_inc(abs_done, 1)

                def softplus_exp(b, r, m0, m1):
                    act.wait_ge(abs_done, 2 * no(b, r) + (1 if m0 == 0 else 2))
                    nc.scalar.activation(du[:, r % 2, m0:m1, :], du[:, r % 2, m0:m1, :], ACT.Exp, scale=-1.0)\
                        .then_inc(exp_done, 1)

                def softplus_one(b, r):
                    s = r % 2
                    act.wait_ge(exp_done, 2 * no(b, r) + 2)
                    nc.scalar.activation(sp_one[:, :, :], du[:, s, :, :], ACT.Copy, bias=1.0).then_inc(one_done, 1)

                def softplus_ln(b, r):
                    act.wait_ge(sp_step, 2 * no(b, r) + 1)
                    nc.scalar.activation(sp_one[:, :, :], sp_one[:, :, :], ACT.Ln).then_inc(ln_done, 1)

                def scan_chunk(b, r, first=False, last=False):
                    c, s = no(b, r), r % 2
                    act.wait_ge(delta_ready, c + 1)
                    for n in range(N):
                        for m in range(MT):
                            i = (c * N + n) * MT + m
                            act.wait_ge(scanned, i + 1)
                            nc.scalar.activation(decay[m], delta[:, s, m, :], ACT.Exp,
                                                 scale=a_neg[:, m, n:n + 1]).then_inc(decay_ready, 1)
                        if last and n == 3:
                            nc.scalar.activation(gres[:, s, :, :], gres[:, s, :, :], ACT.Silu).then_inc(silu_done, 1)
                            nc.scalar.preload_act_table_set(EXP_LN)
                        if n in (0, 1):
                            conv_out(b, r + 1, n)
                        if not last:
                            if n == 4:
                                conv_out(b, r + 1, 2)
                                silus(b, r + 1, True)
                            if n == 6:
                                gres_out(b, r + 1, 0)
                            if n == 7:
                                rows_out(b, r + 1)
                            if n == 8:
                                gres_out(b, r + 1, 1)
                            if n == 9:
                                dt_out(b, r + 1, 0)
                                dt_out(b, r + 1, 1)
                                softplus_abs(b, r + 1, 0, 2)
                            if n == 10:
                                dt_out(b, r + 1, 2)
                                softplus_abs(b, r + 1, 2, MT)
                                softplus_exp(b, r + 1, 0, 2)
                            if n == 11:
                                softplus_exp(b, r + 1, 2, MT)
                        if not first and n == 11:
                            post_norm_out(b, r - 1)
                        if not last and n == 11:
                            softplus_one(b, r + 1)
                        if not first and n == 12:
                            router_exp(b, r - 1)
                        if last:
                            continue
                        if n == 12:
                            gres_out(b, r + 1, 2)
                        if n == 13:
                            softplus_ln(b, r + 1)
                            norm_out(b, r + 2, 0)
                            norm_out(b, r + 2, 1)
                        if n == 14:
                            xin_out(b, r + 2, 0)
                            xin_out(b, r + 2, 1)
                        if n == 15:
                            xin_out(b, r + 2, 2)

                norm_out(0, 0, 0)
                norm_out(0, 0, 1)
                for m in range(MT):
                    xin_out(0, 0, m)
                for m in range(MT):
                    conv_out(0, 0, m)
                silus(0, 0, False)
                gres_out(0, 0, 0)
                rows_out(0, 0)
                gres_out(0, 0, 1)
                for m in range(MT):
                    dt_out(0, 0, m)
                gres_out(0, 0, 2)
                softplus_abs(0, 0, 0, 2)
                softplus_abs(0, 0, 2, MT)
                softplus_exp(0, 0, 0, 2)
                norm_out(0, 1, 0)
                norm_out(0, 1, 1)
                softplus_exp(0, 0, 2, MT)
                softplus_one(0, 0)
                xin_out(0, 1, 0)
                softplus_ln(0, 0)
                xin_out(0, 1, 1)
                xin_out(0, 1, 2)
                scan_chunk(0, 0, first=True)
                with act.Fori(0, BATCH - 1) as b:
                    scan_chunk(b, 1)
                    scan_chunk(b, 2)
                scan_chunk(BATCH - 1, 1, last=True)
                post_norm_out(BATCH - 1, 1)
                router_exp(BATCH - 1, 1)
                act.wait_ge(pad_ready, 1)
                act.wait_ge(table_ready, 1)
                for e in range(E // 2, E):
                    pad_list(act, e)

            @block.tensor
            def _(pe):
                pe.wait_ge(weights_in, 16 * 11)
                pe.wait_ge(diag_ready, 1)

                def claim(use):
                    k, uses = use
                    pe.wait_ge(freed[k], uses + 1)
                    return k

                def moved(b, r, u):
                    k, uses = pre_use(b, r, u)
                    pe.wait_ge(freed[k], uses + 2)

                def turn(b, r, part):
                    pe.wait_ge(pre_norm.norm_done, 2 * no(b, r) + 2)
                    u, c0, rows = (("TA", 0, P), ("TB", P, DH))[part]
                    k = claim(pre_use(b, r, u))
                    settle(pe, passed)
                    for i in range(TPC):
                        mm = nc.tensor.transpose(work[k][0:rows, i * P:(i + 1) * P],
                                                 x1[:, i, c0:c0 + rows], ident[:, :])
                    mm.then_inc(filled[k], 1)

                def project_in(b, r, u, m):
                    if u == "IN0":
                        moved(b, r, "TA")
                        moved(b, r, "TB")
                    k = claim(pre_use(b, r, u))
                    nc.tensor.matmul(work[k][:, :], w_in_a[:, m * P:(m + 1) * P], xn_a[:, :], start=True, stop=False)
                    nc.tensor.matmul(work[k][:, :], w_in_b[:, m * P:(m + 1) * P], xn_b[:, :], start=False, stop=True)\
                        .then_inc(filled[k], 1)

                def convolve(b, r, m):
                    moved(b, r, f"IN{m}")
                    k = claim(pre_use(b, r, f"CONV{m}"))
                    for tap in range(TAPS):
                        mm = nc.tensor.matmul(work[k][:, :], conv_diag[:, m, tap, :], xin[:, m, tap:tap + CH],
                                              start=(tap == 0), stop=(tap == TAPS - 1))
                    mm.then_inc(filled[k], 1)

                def project_x(b, r):
                    c = no(b, r)
                    pe.wait_ge(silu_done, 2 * c + 1)
                    k = claim(pre_use(b, r, "XP"))
                    for m in range(MT):
                        mm = nc.tensor.matmul(work[k][0:XR, :], w_x_sb[:, m, :], u_sb[:, r % 2, m, :],
                                              start=(m == 0), stop=(m == MT - 1))
                    mm.then_inc(filled[k], 1)

                def project_dt(b, r, m):
                    moved(b, r, "XP")
                    k = claim(pre_use(b, r, f"DT{m}"))
                    nc.tensor.matmul(work[k][:, :], w_dt_sb[:, m * P:(m + 1) * P], dt_sb[:, :],
                                     start=True, stop=True).then_inc(filled[k], 1)

                def post_turn(b, r):
                    pe.wait_ge(post_norm.norm_done, 2 * no(b, r) + 2)
                    for what, c0, rows in (("TA", 0, P), ("TB", P, DH)):
                        k = claim(post_use(b, r, what))
                        settle(pe, passed)
                        for i in range(TPC):
                            mm = nc.tensor.transpose(work[k][0:rows, i * P:(i + 1) * P],
                                                     row[:, r % 2, i, c0:c0 + rows], ident[:, :])
                        mm.then_inc(filled[k], 1)

                def route(b, r):
                    for what in ("TA", "TB"):
                        k, uses = post_use(b, r, what)
                        pe.wait_ge(freed[k], uses + 2)
                    k = claim(post_use(b, r, "LOGITS"))
                    for i in range(TPC):
                        for part, (xm, rt) in enumerate(((xm_a, router_a), (xm_b, router_b))):
                            mm = nc.tensor.matmul(work[k][:, i * E:(i + 1) * E], xm[:, i * P:(i + 1) * P], rt[:, :],
                                                  start=(part == 0), stop=(part == 1))
                    mm.then_inc(filled[k], 1)

                def rank(b, r):
                    pe.wait_ge(picked, no(b, r) + 1)
                    k = claim(post_use(b, r, "RANKS"))
                    both = pick[:, 2, :, :].rearrange("p i e -> p (i e)")
                    nc.tensor.matmul(work[k][:, 0:TPC * E], before[:, :], both, start=True, stop=True)
                    nc.tensor.matmul(work[k][:, TPC * E:2 * TPC * E], ones[:, :], both, start=True, stop=True)\
                        .then_inc(filled[k], 1)

                def project_out(b, r, pair):
                    pe.wait_ge(gated, no(b, r) + 1)
                    k = claim(post_use(b, r, f"OUT{pair}"))
                    for i in range(2):
                        t = (2 * pair + i) * P
                        for m in range(MT):
                            mm = nc.tensor.matmul(work[k][:, i * D:(i + 1) * D], yg[:, m, t:t + P],
                                                  w_out_sb[:, m, :], start=(m == 0), stop=(m == MT - 1))
                    mm.then_inc(filled[k], 1)

                def broadcast_b(b, r, n):
                    if n >= N:
                        r, n = r + 1, n - N
                    c = no(b, r)
                    if n == 0:
                        pe.wait_ge(parts_ready, c + 1)
                    pe.wait_ge(dbu_ready, c * N + n + 1)
                    nc.tensor.matmul(b_bc[:, :], sel[:, n, :], b_parts[:, r % 2, :], start=True, stop=True)\
                        .then_inc(b_bc_ready, 1)

                def skip(b, r):
                    c = no(b, r)
                    if not (isinstance(c, int) and c == 0):
                        pe.wait_ge(gated, c)
                    for m in range(MT):
                        nc.tensor.matmul(y_ps[:, m, :], d_diag[:, m, :], u_sb[:, r % 2, m, :], start=True, stop=False)

                def scan_chunk(b, r, first=False, last=False):
                    c = no(b, r)
                    for n in range(N):
                        if n == 0:
                            skip(b, r)
                            broadcast_b(b, r, AHEAD)
                        pe.wait_ge(hc_ready, c * N + n + 3)
                        for m in range(MT):
                            mm = nc.tensor.matmul(y_ps[:, m, :], ident[:, :], hc[:, n % HS, m, :],
                                                  start=False, stop=(n == N - 1))
                        mm.then_inc(hc_added, 1)
                        if not first:
                            if n in (2, 3):
                                project_out(b, r - 1, n - 2)
                            if n == 9:
                                post_turn(b, r - 1)
                        if not last:
                            if n == 1:
                                convolve(b, r + 1, 2)
                            if n == 4:
                                project_in(b, r + 1, "RES0", MT)
                            if n == 5:
                                project_x(b, r + 1)
                            if n == 6:
                                project_in(b, r + 1, "RES1", MT + 1)
                            if n == 7:
                                project_dt(b, r + 1, 0)
                                project_dt(b, r + 1, 1)
                            if n == 8:
                                project_dt(b, r + 1, 2)
                            if n == 10:
                                project_in(b, r + 1, "RES2", MT + 2)
                        if not first and n == 10:
                            route(b, r - 1)
                        if not last:
                            if n == 11:
                                turn(b, r + 2, 0)
                                turn(b, r + 2, 1)
                            if n == 12:
                                project_in(b, r + 2, "IN0", 0)
                                project_in(b, r + 2, "IN1", 1)
                            if n == 13:
                                project_in(b, r + 2, "IN2", 2)
                        if n == 13:
                            if first:
                                k = claim(post_use(b, r - 1, "RANKS"))
                                pe.sem_inc(filled[k], 1)
                                pe.sem_inc(freed[k], 1)
                            else:
                                rank(b, r - 1)
                        if not last and n in (14, 15):
                            convolve(b, r + 2, n - 14)
                        if n > 0 and not (last and n + AHEAD >= N):
                            broadcast_b(b, r, n + AHEAD)

                for part in range(2):
                    turn(0, 0, part)
                for m in range(MT):
                    project_in(0, 0, f"IN{m}", m)
                for m in range(MT):
                    convolve(0, 0, m)
                project_in(0, 0, "RES0", MT)
                project_x(0, 0)
                project_in(0, 0, "RES1", MT + 1)
                for m in range(MT):
                    project_dt(0, 0, m)
                project_in(0, 0, "RES2", MT + 2)
                for part in range(2):
                    turn(0, 1, part)
                for m in range(MT):
                    project_in(0, 1, f"IN{m}", m)
                for m in range(2):
                    broadcast_b(0, 0, m)
                    convolve(0, 1, m)
                broadcast_b(0, 0, 2)
                scan_chunk(0, 0, first=True)
                with pe.Fori(0, BATCH - 1) as b:
                    scan_chunk(b, 1)
                    scan_chunk(b, 2)
                scan_chunk(BATCH - 1, 1, last=True)
                for pair in range(TPC // 2):
                    project_out(BATCH - 1, 1, pair)
                post_turn(BATCH - 1, 1)
                route(BATCH - 1, 1)
                rank(BATCH - 1, 1)

            @block.vector
            def _(dve):
                nc.vector.memset(h_all[:, 0:TPC, :], 0.0).then_inc(h_zero, 1)
                nc.vector.memset(h_all[:, TPC:, :], 0.0).then_inc(h_zero, 1)
                nc.vector.memset(ones[:, :], 1.0)
                nc.vector.memset(row[:, :, :, :], 0.0)
                nc.vector.memset(slot[:, :, :, :], PAST).then_inc(slots_ready, 1)
                dve.wait_ge(iota_ready, 1)
                nc.vector.tensor_copy(run[:, 0, :], list_start[:, :]).then_inc(run_begun, 1)
                dve.wait_ge(run_begun, 1)
                nc.vector.memset(b_parts[:, :, :], 0.0)
                nc.vector.memset(xin[:, :, 0:HALO], 0.0).then_inc(halo_ready, 1)
                for reads in (last_saved, hc_ready):
                    nc.vector.sem_inc(reads, 2)
                nc.vector.sem_inc(scanned, MT)
                nc.vector.sem_inc(hc_added, HS)
                nc.vector.sem_inc(dbu_ready, 1)
                for k in range(2):
                    had = len(range(k, FIRST_USE, 2))
                    nc.vector.sem_inc(filled[k], had)
                    nc.vector.sem_inc(freed[k], had + 1)
                dve.wait_ge(weights_in, 16 * 11)
                for m in range(MT):
                    for tap in range(TAPS):
                        nc.vector.tensor_scalar(conv_diag[:, m, tap, :], ident[:, :], conv_w[:, m, tap:tap + 1],
                                                None, ALU.mult)
                    last_diag = nc.vector.tensor_scalar(d_diag[:, m, :], ident[:, :], d_par[:, m, :], None, ALU.mult)
                last_diag.then_inc(diag_ready, 1)

                x1_tiles = [x1[:, i, :] for i in range(TPC)]

                def norm_source(b, r):
                    return [h_all[:, bass.ds(no(b, r) * TPC + i, 1), :].rearrange("p a d -> p (a d)")
                            for i in range(TPC)]

                def norm_stats(b, r, step):
                    layer_norm_stats(dve, pre_norm, norm_source(b, r) if step == 0 else x1_tiles, 2 * no(b, r) + step)

                def norm_apply(b, r, step):
                    if step == 0 and not (isinstance(b, int) and no(b, r) == 0):
                        pb, pr = (b, r - 1)
                        k, uses = pre_use(pb, pr, "TB")
                        dve.wait_ge(filled[k], uses + 1)
                    layer_norm_apply(dve, pre_norm, norm_source(b, r) if step == 0 else x1_tiles, x1_tiles,
                                     2 * no(b, r) + step)

                def next_halo(b, r):
                    k, uses = pre_use(b, r - 1, "CONV2")
                    dve.wait_ge(filled[k], uses + 1)
                    settle(dve, passed)
                    if r % 2:
                        nc.vector.tensor_copy(xin[:, :, 0:HALO], xin[:, :, CH:CH + HALO]).then_inc(halo_ready, 1)
                    else:
                        nc.vector.memset(xin[:, :, 0:HALO], 0.0).then_inc(halo_ready, 1)

                def split_b(b, r):
                    c, s = no(b, r), r % 2
                    dve.wait_ge(rows_ready, 2 * c + 1)
                    nc.vector.tensor_copy(b_parts[0:N, s, :], b_rows[:, :]).then_inc(split_step, 1)
                    dve.wait_ge(split_step, 4 * c + 1)
                    nc.vector.tensor_tensor(b_rows[:, :], b_rows[:, :], b_parts[0:N, s, :], ALU.subtract)\
                        .then_inc(split_step, 1)
                    dve.wait_ge(split_step, 4 * c + 2)
                    nc.vector.tensor_copy(b_part[:, :], b_rows[:, :])
                    nc.vector.tensor_copy(b_parts[32:32 + N, s, :], b_rows[:, :]).then_inc(split_step, 1)
                    dve.wait_ge(split_step, 4 * c + 3)
                    nc.vector.tensor_tensor(b_rows[:, :], b_rows[:, :], b_part[:, :], ALU.subtract)\
                        .then_inc(split_step, 1)
                    dve.wait_ge(split_step, 4 * c + 4)
                    nc.vector.tensor_copy(b_parts[64:64 + N, s, :], b_rows[:, :]).then_inc(parts_ready, 1)

                def softplus_mid(b, r):
                    c, s = no(b, r), r % 2
                    dve.wait_ge(one_done, c + 1)
                    nc.vector.scalar_tensor_tensor(du[:, s, :, :], sp_one[:, :, :], 1.0, du[:, s, :, :],
                                                   ALU.subtract, ALU.subtract).then_inc(sp_step, 1)
                    dve.wait_ge(sp_step, 2 * c + 1)
                    nc.vector.scalar_tensor_tensor(delta[:, s, :, :], delta[:, s, :, :], 0.0, du[:, s, :, :],
                                                   ALU.max, ALU.subtract).then_inc(sp_step, 1)

                def softplus_end(b, r):
                    c, s = no(b, r), r % 2
                    dve.wait_ge(ln_done, c + 1)
                    dve.wait_ge(sp_step, 2 * c + 2)
                    nc.vector.tensor_tensor(delta[:, s, :, :], delta[:, s, :, :], sp_one[:, :, :], ALU.add)\
                        .then_inc(delta_ready, 1)

                def post_norm_first(b, r):
                    for pair in range(TPC // 2):
                        k, uses = post_use(b, r, f"OUT{pair}")
                        dve.wait_ge(freed[k], uses + 2)
                    settle(dve, passed)
                    layer_norm_stats(dve, post_norm, norm_source(b, r), 2 * no(b, r))

                def post_norm_mid(b, r):
                    c = no(b, r)
                    x3_tiles = [x3[:, i, :] for i in range(TPC)]
                    layer_norm_apply(dve, post_norm, norm_source(b, r), x3_tiles, 2 * c)
                    h = h_all[:, bass.ds(c * TPC, TPC), :]
                    nc.vector.tensor_tensor(h, h, x3[:, :, :], ALU.add).then_inc(residual_added, 1)
                    layer_norm_stats(dve, post_norm, x3_tiles, 2 * c + 1)

                def post_norm_last(b, r):
                    c, s = no(b, r), r % 2
                    if not (isinstance(c, int) and c == 0):
                        dve.wait_ge(scattered[s], 16 * 2 * TPC * (b + (r + 1) // 2))
                    layer_norm_apply(dve, post_norm, [x3[:, i, :] for i in range(TPC)],
                                     [row[:, s, i, 0:D] for i in range(TPC)], 2 * c + 1)

                def router_max(b, r):
                    c = no(b, r)
                    k, uses = post_use(b, r, "LOGITS")
                    dve.wait_ge(filled[k], uses + 1)
                    logits = work[k][:, 0:TPC * E].rearrange("p (i e) -> p i e", e=E)
                    nc.vector.tensor_reduce(col[:, 0, :], logits, AX_X, ALU.max).then_inc(soft_step, 1)
                    dve.wait_ge(soft_step, 2 * c + 1)
                    nc.vector.tensor_tensor(prob[:, 0, :, :], logits,
                                            col[:, 0, :].unsqueeze(2).broadcast_to([P, TPC, E]),
                                            ALU.subtract).then_inc(soft_step, 1)
                    dve.wait_ge(soft_step, 2 * c + 2)
                    settle(dve, freed[k])

                def choose(b, r):
                    c, s = no(b, r), r % 2
                    t = top_step
                    dve.wait_ge(prob_exp, c + 1)
                    nc.vector.tensor_reduce(col[:, 1, :], prob[:, 1, :, :], AX_X, ALU.add).then_inc(t, 1)
                    dve.wait_ge(t, 8 * c + 1)
                    nc.vector.reciprocal(col[:, 2, :], col[:, 1, :]).then_inc(t, 1)
                    dve.wait_ge(t, 8 * c + 2)
                    nc.vector.tensor_tensor(prob[:, 2, :, :], prob[:, 1, :, :],
                                            col[:, 2, :].unsqueeze(2).broadcast_to([P, TPC, E]),
                                            ALU.mult).then_inc(t, 1)
                    dve.wait_ge(t, 8 * c + 3)
                    settle(dve, passed)
                    for i in range(TPC):
                        last = nc.vector.max(top[:, i, :], prob[:, 2, i, :])
                    last.then_inc(t, 1)
                    dve.wait_ge(t, 8 * c + 4)
                    settle(dve, passed)
                    for i in range(TPC):
                        last = nc.vector.max_index(top_i[:, i, :], top[:, i, :], prob[:, 2, i, :])
                    last.then_inc(t, 1)
                    nc.vector.tensor_tensor(col[:, 0, :], top[:, :, 0], top[:, :, 1], ALU.add).then_inc(t, 1)
                    dve.wait_ge(t, 8 * c + 6)
                    nc.vector.reciprocal(col[:, 1, :], col[:, 0, :]).then_inc(t, 1)
                    nc.vector.tensor_copy(row[:, s, :, ROW_E:ROW_E + 2], top_i[:, :, 0:2])
                    nc.vector.tensor_copy(row[:, s, :, ROW_ID:ROW_ID + 1].bitcast(I32),
                                          token_no[:, bass.ds(c * TPC, TPC)].unsqueeze(2)).then_inc(t, 1)
                    dve.wait_ge(t, 8 * c + 8)
                    nc.vector.tensor_tensor(row[:, s, :, ROW_W:ROW_W + 2], top[:, :, 0:2],
                                            col[:, 1, :].unsqueeze(2).broadcast_to([P, TPC, 2]), ALU.mult)
                    for choice in range(2):
                        no_ = expert_no[:, :].unsqueeze(1).broadcast_to([P, TPC, E])
                        last = nc.vector.tensor_tensor(
                            pick[:, choice, :, :], no_,
                            row[:, s, :, ROW_E + choice:ROW_E + choice + 1].broadcast_to([P, TPC, E]), ALU.is_equal)
                    last.then_inc(pick_step, 1)
                    dve.wait_ge(pick_step, c + 1)
                    nc.vector.tensor_tensor(pick[:, 2, :, :], pick[:, 0, :, :], pick[:, 1, :, :], ALU.add)\
                        .then_inc(picked, 1)

                def find_slots(b, r):
                    c, s = no(b, r), r % 2
                    k, uses = post_use(b, r, "RANKS")
                    dve.wait_ge(filled[k], uses + 1)
                    for i in range(TPC):
                        g = c * TPC + i
                        run_now, run_next = (run[:, bass.ds(g + x, 1), :].rearrange("p a e -> p (a e)")
                                             for x in range(2))
                        nc.vector.tensor_tensor(run_next, run_now, work[k][:, (TPC + i) * E:(TPC + i + 1) * E],
                                                ALU.add).then_inc(rank_step, 1)
                        dve.wait_ge(rank_step, 6 * c + i + 1)
                    nc.vector.tensor_tensor(place[:, :, :], run[:, bass.ds(c * TPC, TPC), :],
                                            work[k][:, 0:TPC * E].rearrange("p (i e) -> p i e", e=E),
                                            ALU.add).then_inc(rank_step, 1)
                    dve.wait_ge(rank_step, 6 * c + 5)
                    settle(dve, freed[k])
                    nc.vector.tensor_tensor(placed[:, :, :, :], pick[:, 0:2, :, :],
                                            place[:, :, :].unsqueeze(1).broadcast_to([P, 2, TPC, E]), ALU.mult)\
                        .then_inc(rank_step, 1)
                    dve.wait_ge(rank_step, 6 * c + 6)
                    nc.vector.tensor_reduce(slot_f[:, :, :], placed[:, :, :, :], AX_X, ALU.add).then_inc(slot_step, 1)
                    dve.wait_ge(slot_step, c + 1)
                    nc.vector.tensor_copy(slot[:, s, :, :], slot_f[:, :, :]).then_inc(slots_ready, 1)

                def gate(b, r):
                    c = no(b, r)
                    dve.wait_ge(hc_added, (c + 1) * N + HS)
                    dve.wait_ge(silu_done, 2 * c + (2 if isinstance(c, int) and c == NCH - 1 else 3))
                    nc.vector.tensor_tensor(yg[:, :, :], y_ps[:, :, :], gres[:, r % 2, :, :], ALU.mult)\
                        .then_inc(gated, 1)

                def add_out(b, r, pair):
                    k, uses = post_use(b, r, f"OUT{pair}")
                    dve.wait_ge(filled[k], uses + 1)
                    h = h_all[:, bass.ds(no(b, r) * TPC + 2 * pair, 2), :]
                    nc.vector.tensor_tensor(h, h, work[k][:, 0:2 * D].rearrange("p (a d) -> p a d", a=2),
                                            ALU.add).then_inc(freed[k], 1)

                def scan_chunk(b, r, first=False, last=False):
                    c, s = no(b, r), r % 2
                    dve.wait_ge(du_ready, c + 1)
                    if s == 1:
                        dve.wait_ge(last_saved, (b + 1) * N + 2)
                    for n in range(N):
                        q = c * N + n
                        dve.wait_ge(b_bc_ready, q + 1)
                        if not (first and n == 0):
                            dve.wait_ge(scanned, q * MT)
                        nc.vector.tensor_tensor(
                            dbu[:, n % 2, :, :], du[:, s, :, :],
                            b_bc[:, :].rearrange("p (a t) -> p a t", a=1).broadcast_to([P, MT, CH]),
                            ALU.mult).then_inc(dbu_ready, 1)
                        dve.wait_ge(dbu_ready, q + 2)
                        dve.wait_ge(hc_ready, q + 1)
                        if s == 0:
                            dve.wait_ge(last_saved, (b + r // 2) * N + n + 1)
                        for m in range(MT):
                            dve.wait_ge(decay_ready, q * MT + m + 1)
                            init = 0.0 if s == 0 else h_last[:, m, n:n + 1]
                            nc.vector.tensor_tensor_scan(hst[:, n % 2, m, :], decay[m],
                                                         dbu[:, n % 2, m, :], init, ALU.mult, ALU.add)\
                                .then_inc(scanned, 1)
                        if not first and n == 1:
                            gate(b, r - 1)
                        if not first:
                            if n in (4, 5):
                                add_out(b, r - 1, n - 4)
                            if n == 5:
                                post_norm_first(b, r - 1)
                            if n == 7:
                                post_norm_mid(b, r - 1)
                            if n == 9:
                                post_norm_last(b, r - 1)
                            if n == 13:
                                choose(b, r - 1)
                        if not last:
                            if n == 2:
                                norm_stats(b, r + 2, 0)
                            if n == 3:
                                norm_apply(b, r + 2, 0)
                                norm_stats(b, r + 2, 1)
                            if n == 6:
                                norm_apply(b, r + 2, 1)
                                next_halo(b, r + 2)
                            if n == 10:
                                split_b(b, r + 1)
                            if n == 12:
                                softplus_mid(b, r + 1)
                            if n == 14:
                                softplus_end(b, r + 1)
                        if not first and n == 12:
                            router_max(b, r - 1)
                    if not first:
                        find_slots(b, r - 1)

                for k in range(2):
                    dve.wait_ge(gathered[k], 16 * TPC)
                    for step in range(2):
                        norm_stats(0, k, step)
                        norm_apply(0, k, step)
                    if k == 0:
                        dve.wait_ge(weights_in, 16 * 11)
                next_halo(0, 1)
                split_b(0, 0)
                softplus_mid(0, 0)
                softplus_end(0, 0)
                dve.wait_ge(gathered[2], 16 * (GT - 2 * TPC))
                scan_chunk(0, 0, first=True)
                with dve.Fori(0, BATCH - 1) as b:
                    scan_chunk(b, 1)
                    scan_chunk(b, 2)
                scan_chunk(BATCH - 1, 1, last=True)
                gate(BATCH - 1, 1)
                for pair in range(TPC // 2):
                    add_out(BATCH - 1, 1, pair)
                post_norm_first(BATCH - 1, 1)
                post_norm_mid(BATCH - 1, 1)
                post_norm_last(BATCH - 1, 1)
                router_max(BATCH - 1, 1)
                choose(BATCH - 1, 1)
                find_slots(BATCH - 1, 1)

                steps = [0]

                def step(instruction):
                    steps[0] += 1
                    instruction.then_inc(table_step, 1)
                    dve.wait_ge(table_step, steps[0])

                end = run[:, GT, :]
                step(nc.vector.tensor_tensor(count[:, :], end, list_start[:, :], ALU.subtract))
                step(nc.vector.tensor_tensor(
                    fills[:, :, :], count[:, :].unsqueeze(2).broadcast_to([P, E, TOK // TS]),
                    tile_no[:, 0:TOK // TS].unsqueeze(1).broadcast_to([P, E, TOK // TS]), ALU.is_gt))
                step(nc.vector.tensor_reduce(tiles_of[:, :], fills[:, :, :], AX_X, ALU.add))
                step(nc.vector.tensor_tensor_scan(tile_end[:, :], ones[:, 0:E], tiles_of[:, :], 0.0, ALU.mult, ALU.add))
                step(nc.vector.tensor_tensor(tiles_of[:, :], tile_end[:, :], tiles_of[:, :], ALU.subtract))
                step(nc.vector.scalar_tensor_tensor(tiles_of[:, :], tiles_of[:, :], -float(TS), list_start[:, :],
                                                    ALU.mult, ALU.add))
                step(nc.vector.scalar_tensor_tensor(
                    fit[:, :, :], tile_no[:, :].unsqueeze(2).broadcast_to([P, NT, E]), 1.0 / TS,
                    tile_end[:, :].unsqueeze(1).broadcast_to([P, NT, E]), ALU.mult, ALU.is_ge))
                step(nc.vector.tensor_reduce(te_f[:, :], fit[:, :, :], AX_X, ALU.add))
                step(nc.vector.tensor_scalar(te_i[:, :], te_f[:, :], float(E - 1), None, ALU.min))
                step(nc.vector.tensor_tensor(fit[:, :, :], te_f[:, :].unsqueeze(2).broadcast_to([P, NT, E]),
                                             expert_no[:, :].unsqueeze(1).broadcast_to([P, NT, E]), ALU.is_equal))
                step(nc.vector.tensor_tensor(fit[:, :, :], fit[:, :, :],
                                             tiles_of[:, :].unsqueeze(1).broadcast_to([P, NT, E]), ALU.mult))
                step(nc.vector.tensor_reduce(row_f[:, :], fit[:, :, :], AX_X, ALU.add))
                step(nc.vector.tensor_scalar(idle[:, :], te_f[:, :], float(E), None, ALU.is_lt))
                step(nc.vector.tensor_tensor(idle[:, :], idle[:, :], tile_no[:, :], ALU.mult))
                step(nc.vector.tensor_tensor(row_f[:, :], row_f[:, :], idle[:, :], ALU.add))
                step(nc.vector.tensor_scalar(idle[:, :], te_f[:, :], float(E), float(PAD_ROW), ALU.is_ge, ALU.mult))
                step(nc.vector.tensor_tensor(row_i[:, :], row_f[:, :], idle[:, :], ALU.add))
                nc.vector.tensor_copy(count_i[:, :], end).then_inc(table_ready, 1)

        with ExitStack() as fctx:
            xt = sb("xt", [P, 4, TT, ROW], F32, fctx)
            xt_a = sb("xt_a", [P, 2, TS], F32, fctx)
            xt_b = sb("xt_b", [DH, 2, TS], F32, fctx)
            w1_a = sb("w1_a", [P, 4, DFF], F32, fctx)
            w1_b = sb("w1_b", [DH, 4, DFF], F32, fctx)
            w2_sb = sb("w2_sb", [P, 4, FT, D], F32, fctx)
            hid = sb("hid", [P, 2, FT, TS], F32, fctx)
            share = sb("share", [P, 2, TT, 2], F32, fctx)
            gate_c = sb("gate_c", [P, 2, TT], F32, fctx)
            ys = sb("ys", [P, 2, TT, D], F32, fctx)

            tr = [ps(f"tr{k}", [P, 2 * TS], fctx) for k in range(2)]
            hp = [ps(f"hp{k}", [P, 2 * TS], fctx) for k in range(2)]
            yp = [ps(f"yp{k}", [P, 2 * TS], fctx) for k in range(2)]

            xt_in = [sem(f"xt_in{k}") for k in range(4)]
            w1_in = [sem(f"w1_in{k}") for k in range(4)]
            w2_in = [sem(f"w2_in{k}") for k in range(4)]
            turned = sem("turned")
            xt_moved = sem("xt_moved")
            hid_filled = sem("hid_filled")
            hid_silu = sem("hid_silu")
            y_filled = sem("y_filled")
            share_done = sem("share_done")
            gate_done = sem("gate_done")
            y_gated = sem("y_gated")
            y_sent = sem("y_sent")

            FP = FT // 2
            block2 = fctx.enter_context(nc.Block())

            @block2.sync
            def _(sp):
                def load_rows(q, i):
                    j = q * 4 + i
                    start = sp.value_load(row_i[0:1, bass.ds(j, 1)], min_val=0, max_val=PAD_ROW)
                    sp.dma_start(xt[:, i % 4, :, :], lists[bass.ds(start, TS), :].rearrange("(i p) d -> p i d", p=P))\
                        .then_inc(xt_in[i % 4], 16)

                def load_w1(q, i):
                    j = q * 4 + i
                    e = sp.value_load(te_i[0:1, bass.ds(j, 1)], min_val=0, max_val=E - 1)
                    e_ = bass.ds(e, 1)
                    sp.dma_start(w1_a[:, i:i + 1, :], w1[e_, 0:P, :].rearrange("e d f -> d e f"))\
                        .then_inc(w1_in[i], 16)
                    sp.dma_start(w1_b[:, i:i + 1, :], w1[e_, P:D, :].rearrange("e d f -> d e f"))\
                        .then_inc(w1_in[i], 16)

                def load_w2(q, i):
                    j = q * 4 + i
                    e = sp.value_load(te_i[0:1, bass.ds(j, 1)], min_val=0, max_val=E - 1)
                    sp.dma_start(w2_sb[:, i, :, :],
                                 w2[bass.ds(e, 1), :, :].rearrange("e (f p) d -> p (e f) d", p=P))\
                        .then_inc(w2_in[i], 16)

                load_rows(0, 0)
                load_w1(0, 0)
                load_rows(0, 1)
                load_w2(0, 0)
                load_w1(0, 1)
                load_w2(0, 1)
                for j in (2, 3):
                    load_rows(0, j)
                    load_w1(0, j)
                    load_w2(0, j)

                def ahead(q, i):
                    j = q * 4 + i
                    sp.wait_ge(y_filled, j - 1)
                    settle(sp, passed)
                    load_w1(q, i)
                    load_w2(q, i)
                    sp.wait_ge(y_sent, (j - 3) * TT * 16)
                    settle(sp, passed)
                    load_rows(q, i)

                with sp.Fori(1, NT // 4) as q:
                    for i in range(4):
                        ahead(q, i)

            @block2.gpsimd
            def _(pool):
                def send(q, i):
                    j = q * 4 + i
                    for t in range(TT):
                        pool.wait_ge(y_gated, (j * TT) + t + 3)
                        if not (isinstance(j, int) and j * TT + t == 0):
                            pool.wait_ge(y_sent, (j * TT + t) * 16)
                        settle(pool, passed)
                        nc.gpsimd.indirect_dma_start(
                            out, bass.IndirectOffsetOnAxis(xt[:, i, t, ROW_ID:ROW_ID + 1].bitcast(U32), 0),
                            ys[:, i % 2, t, :], None, bounds_check=TOK - 1, oob_is_err=False,
                            compute_op=ALU.add).then_inc(y_sent, 16)

                for i in range(4):
                    send(0, i)
                with pool.Fori(1, NT // 4) as q:
                    for i in range(4):
                        send(q, i)
                pool.wait_ge(y_sent, NT * TT * 16)

            @block2.scalar
            def _(act):
                def move(q, i):
                    j = q * 4 + i
                    act.wait_ge(turned, j + 1)
                    if not (isinstance(j, int) and j < 2):
                        act.wait_ge(hid_filled, (j - 1) * FP)
                    nc.scalar.activation(xt_a[:, i % 2, :], tr[i % 2][:, 0:TS], ACT.Identity,
                                         scale=gamma[0], bias=beta[0])
                    nc.scalar.activation(xt_b[:, i % 2, :], tr[i % 2][0:DH, TS:2 * TS], ACT.Identity,
                                         scale=gamma[1], bias=beta[1]).then_inc(xt_moved, 1)

                def silu(q, i):
                    j = q * 4 + i
                    act.wait_ge(y_filled, j + 1)
                    for f in range(FP):
                        act.wait_ge(hid_filled, j * FP + f + 1)
                        nc.scalar.activation(hid[:, i % 2, 2 * f:2 * f + 2, :], hp[(i * FP + f) % 2][:, :], ACT.Silu)\
                            .then_inc(hid_silu, 1)

                move(0, 0)
                move(0, 1)
                silu(0, 0)
                silu(0, 1)
                move(0, 2)
                with act.Fori(0, NT // 4 - 1) as q:
                    for i in range(4):
                        silu(q, i + 2) if i < 2 else silu(q + 1, i - 2)
                        move(q, i + 3) if i == 0 else move(q + 1, i - 1)
                silu(NT // 4 - 1, 2)
                move(NT // 4 - 1, 3)
                silu(NT // 4 - 1, 3)

            @block2.tensor
            def _(pe):
                def turn(q, i):
                    j = q * 4 + i
                    pe.wait_ge(xt_in[i], q * 16 + 16)
                    pe.wait_ge(xt_moved, j + 1)
                    settle(pe, passed)
                    for t in range(TT):
                        nc.tensor.transpose(tr[i % 2][:, t * P:(t + 1) * P], xt[:, i, t, 0:P], ident[:, :])
                        mm = nc.tensor.transpose(tr[i % 2][0:DH, TS + t * P:TS + (t + 1) * P], xt[:, i, t, P:D],
                                                 ident[:, :])
                    mm.then_inc(turned, 1)

                def first_product(q, i):
                    j = q * 4 + i
                    pe.wait_ge(xt_moved, j + 3)
                    pe.wait_ge(w1_in[i], (q + 1) * 32)
                    for f in range(FT):
                        if f % 2 == 0:
                            pe.wait_ge(hid_silu, j * FP + f // 2 + 1)
                        h = hp[(i * FP + f // 2) % 2][:, (f % 2) * TS:(f % 2 + 1) * TS]
                        nc.tensor.matmul(h, w1_a[:, i, f * P:(f + 1) * P], xt_a[:, i % 2, :],
                                         start=True, stop=False)
                        mm = nc.tensor.matmul(h, w1_b[:, i, f * P:(f + 1) * P], xt_b[:, i % 2, :],
                                              start=False, stop=True)
                        if f % 2:
                            mm.then_inc(hid_filled, 1)

                def second_product(q, i):
                    j = q * 4 + i
                    pe.wait_ge(w2_in[i], (q + 1) * 16)
                    pe.wait_ge(hid_silu, (j + 1) * FP + 2)
                    pe.wait_ge(y_gated, j * TT + 1)
                    for t in range(TT):
                        for f in range(FT):
                            mm = nc.tensor.matmul(yp[i % 2][:, t * D:(t + 1) * D], hid[:, i % 2, f, t * P:(t + 1) * P],
                                                  w2_sb[:, i, f, :], start=(f == 0), stop=(f == FT - 1))
                    mm.then_inc(y_filled, 1)

                def at_tile(stage, q, i):
                    stage(q, i) if i < 4 else stage(q + 1, i - 4)

                turn(0, 0)
                turn(0, 1)
                first_product(0, 0)
                with pe.Fori(0, NT // 4 - 1) as q:
                    for i in range(4):
                        at_tile(first_product, q, i + 1)
                        at_tile(turn, q, i + 2)
                        second_product(q, i)
                q = NT // 4 - 1
                for i in range(4):
                    if i < 3:
                        first_product(q, i + 1)
                    if i < 2:
                        turn(q, i + 2)
                    second_product(q, i)

            @block2.vector
            def _(dve):
                for reads in (xt_moved, hid_silu, y_filled, y_gated):
                    nc.vector.sem_inc(reads, 2)

                def weigh(q, i):
                    j = q * 4 + i
                    dve.wait_ge(xt_in[i], q * 16 + 16)
                    nc.vector.scalar_tensor_tensor(share[:, i % 2, :, :], xt[:, i, :, ROW_E:ROW_E + 2],
                                                   te_f[:, bass.ds(j, 1)], xt[:, i, :, ROW_W:ROW_W + 2],
                                                   ALU.is_equal, ALU.mult).then_inc(share_done, 1)
                    dve.wait_ge(share_done, j + 1)
                    nc.vector.tensor_reduce(gate_c[:, i % 2, :], share[:, i % 2, :, :], AX_X, ALU.add)\
                        .then_inc(gate_done, 1)
                    dve.wait_ge(gate_done, j + 1)
                    dve.wait_ge(y_filled, j + 3)
                    if not (isinstance(j, int) and j < 2):
                        dve.wait_ge(y_sent, (j - 1) * TT * 16)
                    for t in range(TT):
                        nc.vector.tensor_scalar(ys[:, i % 2, t, :], yp[i % 2][:, t * D:(t + 1) * D],
                                                gate_c[:, i % 2, t:t + 1], None, ALU.mult).then_inc(y_gated, 1)

                for i in range(4):
                    weigh(0, i)
                with dve.Fori(1, NT // 4) as q:
                    for i in range(4):
                        weigh(q, i)


def kernel(**inputs):
    import ml_dtypes
    import concourse.bacc as bacc
    from concourse.bass_utils import run_bass_kernel_spmd

    a = {k: np.asarray(v) for k, v in inputs.items()}

    def tiles(x):
        x = x.reshape(x.shape[0], -1)
        return x.reshape(-1, P, x.shape[1]).transpose(1, 0, 2).reshape(P, -1)

    def halves(x):
        v = np.zeros((P, 2), np.float32)
        v[:, 0] = x[:P]
        v[:DH, 1] = x[P:]
        return v

    c128 = np.concatenate(
        [halves(a["L0_attn_ln_w"]), halves(a["L0_attn_ln_b"]), halves(a["L0_ffn_ln_gamma"]),
         halves(a["L0_ffn_ln_beta"]), tiles(a["L0_attn_conv_w"][:, 0, :]),
         tiles(a["L0_attn_conv_b"]), tiles(a["L0_attn_dt_proj_b"]), tiles(a["L0_attn_D_param"]),
         tiles(a["L0_attn_A_log"])], axis=1)
    xp = a["L0_attn_x_proj_w"].T
    w_x = np.zeros((DI, XR), np.float32)
    w_x[:, DT0:DT0 + R] = xp[:, 0:R]
    w_x[:, B0:B0 + N] = xp[:, R:R + N]
    w_x[:, C0:C0 + N] = xp[:, R + N:R + 2 * N]
    sel = np.zeros((96, N, P), ml_dtypes.bfloat16)
    for part in range(3):
        for n in range(N):
            sel[32 * part + n, n, :] = 1
    arrays = {
        "ids": a["x"].reshape(GT, P).T,
        "emb": a["L0_tok_W"],
        "c128": c128,
        "ident_d": np.eye(P, dtype=np.float32),
        "sel_d": sel,
        "before_d": np.triu(np.ones((P, P), np.float32), 1),
        "w_in": a["L0_attn_in_proj_w"].T,
        "w_x": w_x,
        "w_dt": a["L0_attn_dt_proj_w"].T,
        "w_out": a["L0_attn_out_proj_w"].T,
        "router_w": a["L0_ffn_router_w"],
        "w1": a["L0_ffn_w1"],
        "w2": a["L0_ffn_w2"],
    }
    nc = bacc.Bacc("TRN2", target_bir_lowering=False, num_devices=1)
    fed, args = {}, []
    for name, x in arrays.items():
        fed[name] = np.ascontiguousarray(x)
        args.append(nc.dram_tensor(name, x.shape, mybir.dt.from_np(x.dtype), kind="ExternalInput").ap())
    out = nc.dram_tensor("out", (TOK, D), F32, kind="ExternalOutput").ap()
    c_scratch = nc.dram_tensor("c_scratch", (HALVES, N, CH), F32, kind="Internal").ap()
    lists = nc.dram_tensor("lists", ((E * LIST + TS), ROW), F32, kind="Internal").ap()
    mamba_moe(nc, *args, out, c_scratch, lists)
    r = run_bass_kernel_spmd(nc, [fed], core_ids=[0])
    return r.results[0]["out"].reshape(BATCH, SEQ, D)
```
